# Optimizing a Trainium2 kernel written in Bass

```python
import numpy as np
import jax
import jax.numpy as jnp

def _softmax(x, axis=-1):
    return jax.nn.softmax(x, axis=axis)
def _gelu(x):
    return jax.nn.gelu(x, approximate=True)
def _silu(x):
    return jax.nn.silu(x)
def _sigmoid(x):
    return jax.nn.sigmoid(x)
def _layernorm(x, axis=-1, eps=1e-5):
    m = jnp.mean(x, axis=axis, keepdims=True)
    v = jnp.var(x, axis=axis, keepdims=True)
    return (x - m) / jnp.sqrt(v + eps)
def _scatter_add(tgt, idx, src, axis=0):
    return tgt.at[idx].add(src)
def _segment_sum(src, seg, n):
    return jax.ops.segment_sum(src, seg, n)

kernel_name = 'mk_adj_preln_d4_adj_128_149f54'

def setup_inputs(seed: int = 0):
    np.random.seed(seed)
    _w = jnp.asarray
    def _rec_inputs():
        import jax
        import jax.numpy as jnp
        _gk = jax.random.key(seed)
        x = -0.000929 + 1 * jax.random.normal(jax.random.fold_in(_gk, 1), (8192, 128), jnp.float32)
        _a = jax.random.bernoulli(jax.random.fold_in(_gk, 2), 0.000488281, (8192, 8192))
        adj = _a.astype(jnp.int32)
        return x, adj
    x, adj = _rec_inputs()
    def _L0_gnn_setup():
        import jax, jax.numpy as jnp
        import numpy as np
        from jax import lax
        N = 8192
        D = 128
        CHUNK = 128
        key = jax.random.key(seed)
        k1, k2 = jax.random.split(key)
        x = jax.random.normal(k1, (N, D), dtype=jnp.float32)
        adj = jax.random.randint(k2, (N, N), 0, 2, dtype=jnp.int32)
        return {'x': x, 'adj': adj}
    _L0_gnn_all = _L0_gnn_setup()
    _L0_gnn_in = {k: v for k, v in _L0_gnn_all.items() if k in ()}
    del _L0_gnn_all

    def _L1_gnn_setup():
        import jax
        import jax.numpy as jnp
        import numpy as np
        from jax import lax
        N = 8192
        F = 128
        CHUNK = 64
        key = jax.random.key(seed)
        kx, ka = jax.random.split(key)
        X = jax.random.normal(kx, (N, F), dtype=jnp.float32)
        adj = jax.random.randint(ka, (N, N), 0, 2, dtype=jnp.int32)
        return {'X': X, 'adj': adj}
    _L1_gnn_all = _L1_gnn_setup()
    _L1_gnn_in = {k: v for k, v in _L1_gnn_all.items() if k in ()}
    del _L1_gnn_all

    def _L2_gnn_setup():
        import jax, jax.numpy as jnp
        import numpy as np
        N = 8192
        F_IN = 128
        D = 128
        NEG_SLOPE = 0.2
        MASK_FILL = -9000000000000000.0
        key = jax.random.key(seed)
        k1, k2, k3, k4 = jax.random.split(key, 4)
        A = jax.random.randint(k1, (N, N), 0, 2, dtype=jnp.int32)
        X = jax.random.normal(k2, (N, F_IN), dtype=jnp.float32)
        lim_w = float(np.sqrt(6.0 / (F_IN + D)))
        Ws = jax.random.uniform(k3, (F_IN, D), minval=-lim_w, maxval=lim_w, dtype=jnp.float32)
        lim_a = 1.414 * float(np.sqrt(6.0 / (2 * D + 1)))
        a = jax.random.uniform(k4, (2 * D, 1), minval=-lim_a, maxval=lim_a, dtype=jnp.float32)
        return {'A': A, 'X': X, 'Ws': Ws, 'a': a}
    _L2_gnn_all = _L2_gnn_setup()
    _L2_gnn_in = {k: v for k, v in _L2_gnn_all.items() if k in ('Ws', 'a', )}
    del _L2_gnn_all

    def _L3_gnn_setup():
        import jax, jax.numpy as jnp
        import numpy as np
        N = 12288
        IN_DIM = 128
        OUT_DIM = 128
        LR_SLOPE = 0.01
        NEG_INF = -9e+16
        key = jax.random.key(seed)
        k1, k2, k3, k4 = jax.random.split(key, 4)
        emb_mat = jax.random.normal(k1, (N, IN_DIM), dtype=jnp.float32)
        adj_mat = jax.random.randint(k2, (N, N), 0, 2, dtype=jnp.int32)
        W = jax.random.normal(k3, (OUT_DIM, IN_DIM), dtype=jnp.float32) * (2.0 / (IN_DIM + OUT_DIM)) ** 0.5
        a = jax.random.normal(k4, (2 * OUT_DIM, 1), dtype=jnp.float32) * (2.0 / (2 * OUT_DIM + 1)) ** 0.5
        return {'emb_mat': emb_mat, 'adj_mat': adj_mat, 'W': W, 'a': a}
    _L3_gnn_all = _L3_gnn_setup()
    _L3_gnn_in = {k: v for k, v in _L3_gnn_all.items() if k in ('W', 'a', )}
    del _L3_gnn_all

    return {
        "x": x,
        "adj": adj,
        "L2_gnn_Ws": _L2_gnn_in["Ws"],
        "L2_gnn_a": _L2_gnn_in["a"],
        "L3_gnn_W": _L3_gnn_in["W"],
        "L3_gnn_a": _L3_gnn_in["a"],
    }

def reference(x, adj, L2_gnn_Ws, L2_gnn_a, L3_gnn_W, L3_gnn_a):
    import jax
    import jax.numpy as jnp
    def _L0_gnn_ref(x, adj):
        import jax, jax.numpy as jnp
        import numpy as np
        from jax import lax
        N = 8192
        D = 128
        CHUNK = 128
        n, d = x.shape
        neg = jnp.finfo(x.dtype).min
        adj_chunks = adj.reshape(n // CHUNK, CHUNK, n)

        def step(carry, a):
            mask = a != 0
            masked = jnp.where(mask[:, :, None], x[None, :, :], neg)
            m = jnp.max(masked, axis=1)
            has_nbr = jnp.any(mask, axis=1)
            out = jnp.where(has_nbr[:, None], m, jnp.zeros((), x.dtype))
            return (carry, out)
        _, out = lax.scan(step, None, adj_chunks)
        return out.reshape(n, d)

    def _L1_gnn_ref(X, adj):
        import jax
        import jax.numpy as jnp
        import numpy as np
        from jax import lax
        N = 8192
        F = 128
        CHUNK = 64
        neg = jnp.finfo(X.dtype).min
        mask = adj != 0
        n, f = X.shape

        def body(_, mrows):
            vals = jnp.max(jnp.where(mrows[:, :, None], X[None, :, :], neg), axis=1)
            has_nbr = jnp.any(mrows, axis=1)
            return (None, jnp.where(has_nbr[:, None], vals, jnp.zeros((), X.dtype)))
        _, out = lax.scan(body, None, mask.reshape(n // CHUNK, CHUNK, n))
        return out.reshape(n, f)

    def _L2_gnn_ref(A, X, Ws, a):
        import jax, jax.numpy as jnp
        import numpy as np
        N = 8192
        F_IN = 128
        D = 128
        NEG_SLOPE = 0.2
        MASK_FILL = -9000000000000000.0
        Wh = X @ Ws
        d = Wh.shape[-1]
        e1 = Wh @ a[:d]
        e2 = Wh @ a[d:]
        e = jax.nn.leaky_relu(e1 + e2.T, negative_slope=NEG_SLOPE)
        e = jnp.where(A > 0, e, MASK_FILL)
        attn = jax.nn.softmax(e, axis=1)
        H = attn @ Wh
        return H

    def _L3_gnn_ref(emb_mat, adj_mat, W, a):
        import jax, jax.numpy as jnp
        import numpy as np
        N = 12288
        IN_DIM = 128
        OUT_DIM = 128
        LR_SLOPE = 0.01
        NEG_INF = -9e+16
        out_dim = W.shape[0]
        e_new = emb_mat @ W.T
        a1 = a[:out_dim, :]
        a2 = a[out_dim:, :]
        source_scores = e_new @ a1
        target_scores = e_new @ a2
        e = source_scores + target_scores.T
        e = jax.nn.leaky_relu(e, negative_slope=LR_SLOPE)
        e = jnp.where(adj_mat > 0, e, NEG_INF)
        attention = jax.nn.softmax(e, axis=-1)
        e_transf = attention @ e_new
        return jax.nn.relu(e_transf)

    h = jnp.maximum(_layernorm(x, axis=-1), 0.0)
    x = x + _L0_gnn_ref(h, adj)
    h = jnp.maximum(_layernorm(x, axis=-1), 0.0)
    x = x + _L1_gnn_ref(h, adj)
    h = jnp.maximum(_layernorm(x, axis=-1), 0.0)
    x = x + _L2_gnn_ref(adj, h, L2_gnn_Ws, L2_gnn_a)
    h = jnp.maximum(_layernorm(x, axis=-1), 0.0)
    x = x + _L3_gnn_ref(h, adj, L3_gnn_W, L3_gnn_a)
    return x


_drawn_inputs = setup_inputs


def setup_inputs(seed=0):
    import zlib

    import numpy as np

    out = dict(_drawn_inputs(seed))
    spreads = {}
    factors = {}
    for name, (base, spread) in spreads.items():
        noise = np.random.default_rng([zlib.crc32(name.encode()), seed]).standard_normal(out[name].shape)
        drawn = base * np.exp(spread * noise) if base else spread * noise
        out[name] = jnp.asarray(drawn.astype(out[name].dtype))
    for name, factor in factors.items():
        out[name] = (out[name] * factor).astype(out[name].dtype)
    return out
```

```python
import concourse.bass as bass
from concourse import mybir
from contextlib import ExitStack

P = 128
TILES = 16
SEG = 1024
FOUND = 8
KEEP = 24
REC = 28
HALF = 4
RING = 4
ROW = 132

SLOTS = [20, 8, 7, 6, 6, 5, 5, 4, 4, 4, 3, 3, 3, 2, 2, 2]
AT = [sum(SLOTS[:b]) for b in range(TILES)]
SLOTS_ALL = sum(SLOTS)
WIDE, NARROW = SLOTS[0], SLOTS[1]

LN_EPS = 1e-5
SLOPE = {2: 0.2, 3: 0.01}
FILL = {2: -9000000000000000.0, 3: -9e16}
PAD_SCORE = -1e30


def gnn_kernel(nc, x, adj, w2, a2, w3, a3, out):
    f32, i32, u32, bf16 = mybir.dt.float32, mybir.dt.int32, mybir.dt.uint32, mybir.dt.bfloat16
    ALU, ACT, AX = mybir.AluOpType, mybir.ActivationFunctionType, mybir.AxisListType

    N = x.shape[0]
    GROUPS = N // (P * TILES)
    NT = N // P
    GROUP = P * TILES
    SEGS = N // SEG
    LOADS = SEGS // HALF
    CAND = SEGS * FOUND
    LAYERS = 4
    CLASSES = KEEP + 1

    tab = [nc.dram_tensor(f"table_{n}", (N + 1, P if n < 2 else ROW), f32, kind="Internal").ap() for n in range(LAYERS)]
    scores_dram = nc.dram_tensor("scores_dram", (N,), f32, kind="Internal").ap()
    records = nc.dram_tensor("records", (N, REC), u32, kind="Internal").ap()

    ctx = ExitStack()
    with ctx:
        def sb(name, shape, dt):
            return ctx.enter_context(nc.sbuf_tensor(name, shape, dt))

        def pb(name, shape, dt):
            return ctx.enter_context(nc.psum_tensor(name, shape, dt))

        def sem(name):
            return ctx.enter_context(nc.semaphore(name))

        arena = sb("arena", [P, RING * HALF * (SEG + FOUND)], i32)
        ring = arena[:, :].rearrange("p (r s c) -> p r s c", r=RING, s=HALF)
        after = arena[:, :].bitcast(f32)
        place_t = after[:, 0:NT * P].rearrange("p (t i) -> p t i", t=NT)
        o = NT * P
        wh_rows = after[:, o:o + TILES * ROW].rearrange("p (t f) -> p t f", t=TILES)
        o += TILES * ROW
        h_t = after[:, o:o + 4 * P]
        o += 4 * P
        tile_of = after[:, o:o + NT * TILES].rearrange("p (t a) -> p t a", t=NT)
        o += NT * TILES
        e1_pick = after[:, o:o + NT * TILES].rearrange("p (t a) -> p t a", t=NT)
        o += NT * TILES
        spot = after[:, o:o + 8 * P].rearrange("p (k i) -> p k i", k=8)
        o += 8 * P

        checked_out = sb("checked_out", [P, HALF, SEG], mybir.dt.uint8)
        X = sb("X", [P, NT, P], f32)
        G = sb("G", [P, SLOTS_ALL * ROW], f32)
        H = sb("H", [P, TILES, P], f32)
        Q = sb("Q", [P, 2, GROUP], f32)
        iota_group = sb("iota_group", [P, GROUP], f32)
        lists = sb("lists", [P, GROUPS, TILES, REC], u32)
        agg = sb("agg", [P, 2, P], f32)

        found = sb("found", [P, 2, CAND], u32)
        key_a = sb("key_a", [P, CAND], f32)
        key_b = sb("key_b", [P, CAND], f32)
        seg_base = sb("seg_base", [P, CAND], f32)
        ones8 = sb("ones8", [P, FOUND], f32)
        best = sb("best", [P, TILES, KEEP], f32)
        uncovered = sb("uncovered", [P, TILES, KEEP], bf16)
        full_seg = sb("full_seg", [P, SEGS], f32)
        deg = sb("deg", [P, TILES], f32)
        class_of = sb("class_of", [P, CLASSES, TILES], bf16)
        is_class = sb("is_class", [P, CLASSES, TILES], bf16)
        ahead = sb("ahead", [P, CLASSES * TILES], f32)
        picked = sb("picked", [P, CLASSES, TILES], f32)
        cells = picked[:, :, :].rearrange("p d t -> p (d t)")[:, 0:TILES * KEEP].rearrange("p (t k) -> p t k", t=TILES)
        rank = sb("rank", [P, TILES], f32)
        rank_int = sb("rank_int", [P, TILES], u32)
        rank_hi = sb("rank_hi", [P, TILES], u32)
        rank_lo = sb("rank_lo", [P, TILES], u32)
        rank_at = sb("rank_at", [P, TILES], u32)
        target = sb("target", [P, TILES], u32)
        group_base = sb("group_base", [P, GROUPS], f32)
        rec_out = sb("rec_out", [P, TILES, REC], u32)
        idx_wide = sb("idx_wide", [P, WIDE], u32)
        idx_rest = sb("idx_rest", [P, TILES, NARROW], u32)
        place = sb("place", [P, NT], f32)
        alone = sb("alone", [P, NT], f32)
        in_tile = sb("in_tile", [P, NT], f32)
        tile_no = sb("tile_no", [P, NT], f32)
        place_lo = sb("place_lo", [P, NT], u32)
        place_hi = sb("place_hi", [P, NT], u32)

        stats = sb("stats", [P, TILES, 6], f32)
        mean_var = sb("mean_var", [P, TILES, 2], f32)
        std = sb("std", [P, TILES], f32)
        rstd = sb("rstd", [P, TILES], f32)
        shift = sb("shift", [P, TILES], f32)
        eps = sb("eps", [P, 1], f32)
        minus_half = sb("minus_half", [P, 1], f32)

        score = sb("score", [P, 2, WIDE], f32)
        leaky = sb("leaky", [P, 2, WIDE], f32)
        prob = sb("prob", [P, 2, WIDE], f32)
        weight = sb("weight", [P, WIDE], f32)
        neg_max = sb("neg_max", [P, 2], f32)
        den = sb("den", [P, 2], f32)
        rden = sb("rden", [P, 2], f32)
        num = sb("num", [P, P], f32)
        mean_wh = sb("mean_wh", [P, P], f32)
        e1_by_row = sb("e1_by_row", [P, NT], f32)
        e1 = sb("e1", [P, NT], f32)

        sums = sb("sums", [P, NT * LOADS], f32)
        odd_sums = sb("odd_sums", [P, NT * LOADS], f32)
        stair = sb("stair", [P, GROUPS], f32)
        faults = sb("faults", [P, 4], f32)
        fault = sb("fault", [P, 1], f32)
        flag = sb("flag", [P, 1], i32)

        diff = sb("diff", [P, P], f32)
        ident = sb("ident", [P, P], f32)
        before = sb("before", [P, P], bf16)
        ones_b = sb("ones_b", [P, P], bf16)
        ones_f = sb("ones_f", [P, P], f32)
        zeros_b = sb("zeros_b", [P, 512], bf16)
        pad_row = sb("pad_row", [1, ROW], f32)
        pad_zero = sb("pad_zero", [1, P], f32)
        w_in = {L: sb(f"w_in{L}", [P, P], f32) for L in (2, 3)}
        w_t2 = sb("w_t2", [P, P], f32)
        w_aug = {L: sb(f"w_aug{L}", [P, P + 2], f32) for L in (2, 3)}
        a_cols = {L: sb(f"a_cols{L}", [P, 2], f32) for L in (2, 3)}

        U = [pb(f"U{c}", [P, 512], f32) for c in range(4)]
        TR = pb("TR", [P, 512], f32)
        WH = [pb(f"WH{c}", [P, 512], f32) for c in range(2)]
        MEAN = pb("MEAN", [P, 512], f32)

        s_x = [sem(f"s_x{g}") for g in range(GROUPS)]
        s_w = sem("s_w")
        s_iota = sem("s_iota")
        s_const = sem("s_const")
        s_pads = sem("s_pads")
        s_own = sem("s_own")
        s_adj = [sem(f"s_adj{r}") for r in range(RING)]
        s_found = sem("s_found")
        s_checked = sem("s_checked")
        s_class = sem("s_class")
        s_counts = sem("s_counts")
        s_target = sem("s_target")
        s_rec = sem("s_rec")
        s_lists = sem("s_lists")
        s_idx_wide = sem("s_idx_wide")
        s_idx_rest = sem("s_idx_rest")
        s_gath = [sem(f"s_gath{b}") for b in range(TILES)]
        s_agg = sem("s_agg")
        s_back = sem("s_back")
        s_added = sem("s_added")
        s_var = sem("s_var")
        s_std = sem("s_std")
        s_ln = sem("s_ln")
        s_h = sem("s_h")
        s_tab = [sem(f"s_tab{n}") for n in range(LAYERS)]
        s_tr = sem("s_tr")
        s_ht = sem("s_ht")
        s_wh = sem("s_wh")
        s_wt = sem("s_wt")
        s_e1r = sem("s_e1r")
        s_mean = sem("s_mean")
        s_meanused = sem("s_meanused")
        s_e1 = sem("s_e1")
        s_e1used = sem("s_e1used")
        s_spot = sem("s_spot")
        s_spot_t = sem("s_spot_t")
        s_place_t = sem("s_place_t")
        s_scores = sem("s_scores")
        s_prob = sem("s_prob")
        s_wprep = sem("s_wprep")
        s_wcopy = sem("s_wcopy")
        s_flt = sem("s_flt")
        s_fltsum = sem("s_fltsum")
        s_flag = sem("s_flag")
        s_out = sem("s_out")

        d_x = sem("d_x")
        d_var = sem("d_var")
        d_std = sem("d_std")
        d_ln = sem("d_ln")
        d_h = sem("d_h")
        d_pe = sem("d_pe")
        d_cp = sem("d_cp")
        d_tab = sem("d_tab")
        d_e2 = sem("d_e2")
        d_adj = sem("d_adj")
        d_scores = sem("d_scores")
        d_prob = sem("d_prob")
        d_rows = [sem(f"d_rows{i}") for i in range(2)]
        d_used = [sem(f"d_used{i}") for i in range(2)]
        d_tile = sem("d_tile")
        d_out = sem("d_out")

        block = ctx.enter_context(nc.Block())

        d_edges = arena[:, 0:N]
        d_target = after[:, N:2 * N]
        d_weight = G[:, 0:N]
        d_chunk = [H[:, :, :], Q[:, 1, :].rearrange("p (k f) -> p k f", f=P)]
        d_prod = Q[:, 0, :].rearrange("p (k f) -> p k f", f=P)
        CHUNK = TILES
        PAIRS = N // (2 * CHUNK)

        def tab_count(L, t):
            return (L * NT + t) if L < 2 else (2 * NT + 2 * ((L - 2) * NT + t))

        def region(b, width):
            at = AT[b] * ROW
            return G[:, at:at + SLOTS[b] * width]

        def turn(L, g, b):
            return (L * GROUPS + g) * TILES + b

        def made(L, g):
            return L * GROUPS + g

        @block.sync
        def _(sp):
            sp.wait_ge(s_const, 1)
            for h in range(NT * LOADS):
                if h >= RING:
                    sp.wait_ge(s_found, h - RING + 1)
                    sp.wait_ge(s_checked, h - RING + 1)
                t, part = h // LOADS, h % LOADS
                src = adj[t * P:(t + 1) * P, part * HALF * SEG:(part + 1) * HALF * SEG]
                sp.dma_start(ring[:, h % RING, :, 0:SEG],
                             src.rearrange("p (s c) -> p s c", s=HALF)).then_inc(s_adj[h % RING], 16)
            for g in range(GROUPS):
                sp.wait_ge(s_added, 4 * (3 * GROUPS + g + 1))
                sp.dma_start(out[g * GROUP:(g + 1) * GROUP, :].rearrange("(t p) f -> p t f", p=P),
                             X[:, g * TILES:(g + 1) * TILES, :]).then_inc(s_out, 16)
            sp.wait_ge(s_out, 16 * GROUPS)

            with sp.If(sp.value_load(flag[0:1, 0:1], min_val=0, max_val=1) > 0):
                sp.dma_start(X[:, :, :], x.rearrange("(t p) f -> p t f", p=P)).then_inc(d_x, 16)
                for L in range(LAYERS):
                    sp.wait_ge(d_tab, 16 * tab_count(L, NT))
                    if L >= 2:
                        sp.dma_start(d_target, scores_dram.rearrange("(o n) -> o n", o=1).broadcast_to([P, N])
                                     ).then_inc(d_e2, 16)
                    with sp.Fori(0, NT) as t:
                        sp.wait_ge(d_tile, t + (L * NT + 1))
                        sp.dma_start(d_edges, adj[bass.ds(t * P, P), :]).then_inc(d_adj, 16)
                        with sp.Fori(0, PAIRS) as c:
                            for i in range(2):
                                sp.wait_ge(d_used[i], t * PAIRS + c + (L * NT * PAIRS + 1))
                                rows = tab[L][bass.ds(c * (2 * CHUNK) + i * CHUNK, CHUNK), 0:P]
                                sp.dma_start(d_chunk[i], rows.unsqueeze(0).broadcast_to([P, CHUNK, P])
                                             ).then_inc(d_rows[i], 16)
                sp.wait_ge(d_tile, LAYERS * NT + 1)
                sp.dma_start(out.rearrange("(t p) f -> p t f", p=P), X[:, :, :]).then_inc(d_out, 16)
                sp.wait_ge(d_out, 16)

        @block.gpsimd
        def _(pool):
            nc.gpsimd.iota(iota_group[:, :], [[1, GROUP]], base=0, channel_multiplier=0,
                           allow_small_or_imprecise_dtypes=True).then_inc(s_iota, 1)
            nc.gpsimd.iota(seg_base[:, :].rearrange("p (s k) -> p s k", s=SEGS), [[-SEG, SEGS], [0, FOUND]], base=N,
                           channel_multiplier=0, allow_small_or_imprecise_dtypes=True).then_inc(s_iota, 1)
            nc.gpsimd.iota(class_of[:, :, :], [[-1, CLASSES], [0, TILES]], base=KEEP, channel_multiplier=0,
                           allow_small_or_imprecise_dtypes=True).then_inc(s_iota, 1)
            nc.gpsimd.iota(group_base[:, :], [[GROUP, GROUPS]], base=0, channel_multiplier=0,
                           allow_small_or_imprecise_dtypes=True).then_inc(s_iota, 1)
            nc.gpsimd.iota(diff[:, :], [[1, P]], base=0, channel_multiplier=-1,
                           allow_small_or_imprecise_dtypes=True).then_inc(s_iota, 1)
            nc.gpsimd.iota(target[:, :], [[P, TILES]], base=0, channel_multiplier=1).then_inc(s_iota, 1)

            def gather(L, g):
                table, width = tab[L], (P if L < 2 else ROW)
                for b in range(TILES):
                    n = turn(L, g, b)
                    if b == 0:
                        pool.wait_ge(s_idx_wide, L * GROUPS + g + 1)
                    if b == 1:
                        pool.wait_ge(s_idx_rest, L * GROUPS + g + 1)
                    if n >= TILES:
                        pool.wait_ge(s_agg, n - TILES + 1)
                    dst = region(b, width)
                    for k in range(SLOTS[b]):
                        idx = idx_wide[:, k:k + 1] if b == 0 else idx_rest[:, b, k:k + 1]
                        pool.indirect_dma_start(dst[:, k * width:(k + 1) * width], None, table,
                                                bass.IndirectOffsetOnAxis(ap=idx, axis=0), bounds_check=N,
                                                oob_is_err=False).then_inc(s_gath[b], 16)

            def scatter_lists(g):
                pool.wait_ge(s_target, g + 1)
                for b in range(TILES):
                    pool.indirect_dma_start(records, bass.IndirectOffsetOnAxis(ap=target[:, b:b + 1], axis=0),
                                            rec_out[:, b, :], None, bounds_check=N - 1,
                                            oob_is_err=False).then_inc(s_rec, 16)
                pool.wait_ge(s_rec, 16 * TILES * (g + 1))
                pool.dma_start(lists[:, g, :, :].rearrange("p t r -> p (t r)"),
                               records[g * GROUP:(g + 1) * GROUP, :].rearrange("(p t) r -> p (t r)", p=P)
                               ).then_inc(s_lists, 16)

            for g in range(GROUPS):
                scatter_lists(g)
                if g == 0:
                    pool.wait_ge(s_pads, 16 * LAYERS)
                    pool.wait_ge(s_tab[0], 16 * GROUPS)
                gather(0, g)
            for L in range(1, LAYERS):
                pool.wait_ge(s_tab[L], 16 * GROUPS)
                for g in range(GROUPS):
                    gather(L, g)

        @block.scalar
        def _(act):
            for g in range(GROUPS):
                act.dma_start(X[:, g * TILES:(g + 1) * TILES, :],
                              x[g * GROUP:(g + 1) * GROUP, :].rearrange("(t p) f -> p t f", p=P)
                              ).then_inc(s_x[g], 16)
            act.dma_start(w_in[2][:, :], w2).then_inc(s_w, 16)
            act.dma_start(w_aug[2][:, 0:P], w2).then_inc(s_w, 16)
            act.dma_start(w_in[3][:, :], w3).then_inc(s_w, 16)
            for L, a in ((2, a2), (3, a3)):
                act.dma_start(a_cols[L][:, 0:1], a[P:2 * P, :]).then_inc(s_w, 16)
                act.dma_start(a_cols[L][:, 1:2], a[0:P, :]).then_inc(s_w, 16)
            act.wait_ge(s_const, 1)
            for L in range(LAYERS):
                act.dma_start(tab[L][N:N + 1, :], pad_zero[0:1, :] if L < 2 else pad_row[0:1, :]).then_inc(s_pads, 16)

            def check(h):
                act.wait_ge(s_adj[h % RING], 16 * (h // RING + 1))
                if h:
                    act.wait_ge(s_checked, h)
                nc.scalar.activation(checked_out[:, :, :], ring[:, h % RING, :, 0:SEG], ACT.Square,
                                     bias=minus_half[:, 0:1], accum_out=sums[:, h:h + 1]).then_inc(s_checked, 1)

            def table_rows(L, g):
                q = made(L, g)
                act.wait_ge(s_var, q + 1)
                nc.scalar.activation(std[:, :], mean_var[:, :, 1], ACT.Sqrt, bias=eps[:, 0:1]).then_inc(s_std, 1)
                act.wait_ge(s_ln, q + 1)
                if q:
                    pL, pg = (q - 1) // GROUPS, (q - 1) % GROUPS
                    if pL < 2:
                        act.wait_ge(s_tab[pL], 16 * (pg + 1))
                    else:
                        act.wait_ge(s_tr, 4 * ((pL - 2) * GROUPS + pg + 1))
                for t in range(TILES):
                    last = nc.scalar.activation(H[:, t, :], X[:, g * TILES + t, :], ACT.Relu,
                                                bias=shift[:, t:t + 1], scale=rstd[:, t:t + 1])
                last.then_inc(s_h, 1)
                rows = tab[L][g * GROUP:(g + 1) * GROUP, :].rearrange("(t p) f -> p t f", p=P)
                if L < 2:
                    act.wait_ge(s_h, q + 1)
                    act.dma_start(rows, H[:, :, :]).then_inc(s_tab[L], 16)
                    return
                m = (L - 2) * GROUPS + g
                for c in range(4):
                    act.wait_ge(s_tr, 4 * m + c + 1)
                    if 4 * m + c:
                        act.wait_ge(s_wh, 2 * (4 * m + c))
                    nc.scalar.copy(h_t[:, :], TR[:, :]).then_inc(s_ht, 1)
                    for half in range(2):
                        k = 2 * (4 * m + c) + half
                        act.wait_ge(s_wh, k + 1)
                        if c == 0 and half == 0 and m:
                            act.wait_ge(s_tab[2 + (m - 1) // GROUPS], 16 * ((m - 1) % GROUPS + 1))
                            act.wait_ge(s_mean, m)
                            act.wait_ge(s_e1r, m)
                        src = WH[half][:, 0:2 * ROW].rearrange("p (t f) -> p t f", t=2)[:, :, 0:P + 2]
                        nc.scalar.copy(wh_rows[:, 4 * c + 2 * half:4 * c + 2 * half + 2, 0:P + 2], src).then_inc(s_wt, 1)
                act.wait_ge(s_wt, 8 * (m + 1))
                act.dma_start(rows, wh_rows[:, :, :]).then_inc(s_tab[L], 16)
                if g == 0 and L == 3:
                    act.wait_ge(s_e1, GROUPS)
                nc.scalar.copy(e1_by_row[:, g * TILES:(g + 1) * TILES], wh_rows[:, :, P + 1]).then_inc(s_e1r, 1)

            act.wait_ge(s_wprep, 1)
            nc.scalar.copy(w_t2[:, :], TR[:, 0:P])
            nc.scalar.copy(w_aug[3][:, 0:P], TR[:, P:2 * P]).then_inc(s_wcopy, 1)
            act.wait_ge(s_wprep, 2)
            nc.scalar.copy(w_aug[2][:, P:P + 2], WH[0][:, 0:2])
            nc.scalar.copy(w_aug[3][:, P:P + 2], WH[0][:, 2:4]).then_inc(s_wcopy, 1)

            for g in range(GROUPS):
                for t in range(TILES):
                    for part in range(LOADS):
                        check((g * TILES + t) * LOADS + part)
                    if g == 0 and t % (TILES // GROUPS) == TILES // GROUPS - 1:
                        table_rows(0, t // (TILES // GROUPS))
                if g:
                    table_rows(1, g - 1)
            table_rows(1, GROUPS - 1)
            for L in range(1, LAYERS):
                for g in range(GROUPS):
                    if L == 1 and g == 0:
                        for r in range(NT // 4):
                            act.wait_ge(s_spot_t, r + 1)
                            nc.scalar.copy(place_t[:, 4 * r:4 * r + 4, :].rearrange("p t i -> p (t i)"),
                                           TR[:, :]).then_inc(s_place_t, 1)
                    if L >= 2:
                        for b in range(TILES):
                            m = turn(L - 2, g, b)
                            act.wait_ge(s_scores, m + 1)
                            k = SLOTS[b]
                            nc.scalar.activation(prob[:, b % 2, 0:k], leaky[:, b % 2, 0:k], ACT.Exp,
                                                 bias=neg_max[:, b % 2:b % 2 + 1],
                                                 accum_out=den[:, b % 2:b % 2 + 1]).then_inc(s_prob, 1)
                    if L < 3:
                        table_rows(L + 1, g)

            act.wait_ge(s_out, 16 * GROUPS)
            with act.If(act.value_load(flag[0:1, 0:1], min_val=0, max_val=1) > 0):
                act.sem_inc(d_h, 1)
                for L in range(LAYERS):
                    with act.Fori(0, NT) as t:
                        act.wait_ge(d_var, t + (L * NT + 1))
                        nc.scalar.activation(std[:, 0:1], mean_var[:, 0, 1:2], ACT.Sqrt,
                                             bias=eps[:, 0:1]).then_inc(d_std, 1)
                        act.wait_ge(d_ln, t + (L * NT + 1))
                        nc.scalar.activation(H[:, 0, :], X[:, bass.ds(t, 1), :].rearrange("p t f -> p (t f)"), ACT.Relu,
                                             bias=shift[:, 0:1], scale=rstd[:, 0:1]).then_inc(d_h, 1)
                        act.wait_ge(d_h, t + (L * NT + 2))
                        if L < 2:
                            act.dma_start(tab[L][bass.ds(t * P, P), :], H[:, 0, :]).then_inc(d_tab, 16)
                            act.wait_ge(d_tab, 16 * t + 16 * (tab_count(L, 0) + 1))
                        else:
                            m = (L - 2) * NT
                            act.wait_ge(d_pe, 2 * t + (2 * m + 1))
                            nc.scalar.copy(h_t[:, 0:P], TR[:, 0:P]).then_inc(d_cp, 1)
                            act.wait_ge(d_pe, 2 * t + (2 * m + 2))
                            nc.scalar.copy(e1_by_row[:, bass.ds(t, 1)], WH[0][:, P + 1:P + 2])
                            nc.scalar.copy(wh_rows[:, 0, 0:P + 2], WH[0][:, 0:P + 2]).then_inc(d_cp, 1)
                            act.wait_ge(d_cp, 2 * t + (2 * m + 2))
                            act.dma_start(tab[L][bass.ds(t * P, P), 0:P + 2], wh_rows[:, 0, 0:P + 2]).then_inc(d_tab, 16)
                            act.dma_start(scores_dram[bass.ds(t * P, P)].unsqueeze(1), wh_rows[:, 0, P:P + 1]
                                          ).then_inc(d_tab, 16)
                            act.wait_ge(d_tab, 32 * t + 16 * (tab_count(L, 0) + 2))
                    if L >= 2:
                        with act.Fori(0, NT) as t:
                            act.wait_ge(d_scores, t + ((L - 2) * NT + 1))
                            nc.scalar.activation(d_weight, d_weight, ACT.Exp, bias=neg_max[:, 0:1],
                                                 accum_out=den[:, 0:1]).then_inc(d_prob, 1)

        @block.tensor
        def _(pe):
            pe.wait_ge(s_w, 16 * 7)
            pe.wait_ge(s_const, 1)
            nc.tensor.transpose(TR[:, 0:P], w_in[2][:, :], ident[:, :])
            nc.tensor.transpose(TR[:, P:2 * P], w_in[3][:, :], ident[:, :]).then_inc(s_wprep, 1)
            pe.wait_ge(s_wcopy, 1)
            nc.tensor.matmul(WH[0][:, 0:2], w_t2[:, :], a_cols[2][:, :], start=True, stop=True)
            nc.tensor.matmul(WH[0][:, 2:4], w_in[3][:, :], a_cols[3][:, :], start=True, stop=True).then_inc(s_wprep, 1)
            pe.wait_ge(s_wcopy, 2)

            def rank_counts(g):
                pe.wait_ge(s_class, g + 1)
                oh = is_class[:, :, :].rearrange("p d t -> p (d t)")
                nc.tensor.matmul(WH[0][:, 0:CLASSES * TILES], before[:, :], oh, start=True, stop=True)
                nc.tensor.matmul(WH[1][:, 0:CLASSES * TILES], ones_b[:, :], oh, start=True,
                                 stop=True).then_inc(s_counts, 1)

            def put_back(L, g, b):
                n = turn(L, g, b)
                if b == 0:
                    if n:
                        pe.wait_ge(s_added, 4 * (L * GROUPS + g))
                    for c in range(4):
                        nc.tensor.matmul(U[c][:, :], zeros_b[:, 0:P], zeros_b[:, :], start=True, stop=False,
                                         skip_group_check=True)
                pe.wait_ge(s_agg, n + 1)
                for a in range(TILES):
                    last = nc.tensor.matmul(U[a // 4][:, (a % 4) * P:(a % 4 + 1) * P],
                                            Q[:, b % 2, a * P:(a + 1) * P], agg[:, b % 2, :], start=False,
                                            stop=(b == TILES - 1), skip_group_check=True)
                last.then_inc(s_back, 1)

            def project(L, g):
                m = (L - 2) * GROUPS + g
                q = made(L, g)
                pe.wait_ge(s_h, q + 1)
                if m == 0:
                    pe.wait_ge(s_place_t, NT // 4)
                if g == 0 and L == 3:
                    pe.wait_ge(s_e1used, 1)
                for c in range(4):
                    if 4 * m + c:
                        pe.wait_ge(s_ht, 4 * m + c)
                    for j in range(4):
                        last = nc.tensor.transpose(TR[:, j * P:(j + 1) * P], H[:, 4 * c + j, :], ident[:, :])
                    last.then_inc(s_tr, 1)
                    pe.wait_ge(s_ht, 4 * m + c + 1)
                    for half in range(2):
                        k = 2 * (4 * m + c) + half
                        if k >= 2:
                            pe.wait_ge(s_wt, k - 1)
                        for j in range(2):
                            last = nc.tensor.matmul(WH[half][:, j * ROW:j * ROW + P + 2],
                                                    h_t[:, (2 * half + j) * P:(2 * half + j + 1) * P],
                                                    w_aug[L][:, :], start=True, stop=True)
                        last.then_inc(s_wh, 1)
                pe.wait_ge(s_wt, 8 * (m + 1))
                if g == 0 and L == 3:
                    pe.wait_ge(s_meanused, 1)
                for t in range(TILES):
                    last = nc.tensor.matmul(MEAN[:, 0:P], ones_f[:, :], wh_rows[:, t, 0:P],
                                            start=(g == 0 and t == 0), stop=(g == GROUPS - 1 and t == TILES - 1))
                last.then_inc(s_mean, 1)

            for g in range(GROUPS):
                if g:
                    for b in range(TILES):
                        put_back(0, g - 1, b)
                rank_counts(g)
            for b in range(TILES):
                put_back(0, GROUPS - 1, b)
            pe.wait_ge(s_flt, 1)
            nc.tensor.matmul(MEAN[:, 0:1], ones_f[:, :], fault[:, :], start=True, stop=True).then_inc(s_fltsum, 1)
            for L in range(1, LAYERS):
                if L >= 2:
                    pe.wait_ge(s_e1r, (L - 1) * GROUPS)
                    for g in range(GROUPS):
                        bank = (TR, WH[0])[g // 2]
                        pe.wait_ge(s_wt, 8 * (L - 1) * GROUPS)
                        for b in range(TILES):
                            at = (g % 2) * 256 + b * TILES
                            last = nc.tensor.matmul(bank[:, at:at + TILES], place_t[:, g * TILES + b, :],
                                                    e1_by_row[:, g * TILES:(g + 1) * TILES], start=True, stop=True)
                        last.then_inc(s_e1, 1)
                for g in range(GROUPS):
                    for b in range(TILES):
                        put_back(L, g, b)
                        if L == 1 and g == 0:
                            for r in range(b * NT // 64, (b + 1) * NT // 64):
                                pe.wait_ge(s_spot, r + 1)
                                if r:
                                    pe.wait_ge(s_place_t, r)
                                for j in range(4):
                                    last = nc.tensor.transpose(TR[:, j * P:(j + 1) * P], spot[:, 4 * (r % 2) + j, :],
                                                               ident[:, :])
                                last.then_inc(s_spot_t, 1)
                    if L < 3:
                        project(L + 1, g)

            pe.wait_ge(s_out, 16 * GROUPS)
            with pe.If(pe.value_load(flag[0:1, 0:1], min_val=0, max_val=1) > 0):
                for L in (2, 3):
                    with pe.Fori(0, NT) as t:
                        pe.wait_ge(d_h, t + (L * NT + 2))
                        nc.tensor.transpose(TR[:, 0:P], H[:, 0, :], ident[:, :]).then_inc(d_pe, 1)
                        pe.wait_ge(d_cp, 2 * t + (2 * (L - 2) * NT + 1))
                        nc.tensor.matmul(WH[0][:, 0:P + 2], h_t[:, 0:P], w_aug[L][:, :], start=True,
                                         stop=True).then_inc(d_pe, 1)

        @block.vector
        def _(dve):
            own = [0]

            def step(ins):
                own[0] += 1
                ins.then_inc(s_own, 1)
                return own[0]

            nc.vector.memset(ones8[:, :], 1.0)
            nc.vector.memset(ring[:, :, :, SEG:SEG + FOUND], 1)
            nc.vector.memset(minus_half[:, :], -0.5)
            nc.vector.memset(eps[:, :], LN_EPS)
            nc.vector.memset(zeros_b[:, :], 0.0)
            nc.vector.memset(ones_b[:, :], 1.0)
            nc.vector.memset(ones_f[:, :], 1.0)
            nc.vector.memset(full_seg[:, :], 0.0)
            nc.vector.memset(pad_zero[:, :], 0.0)
            nc.vector.memset(pad_row[:, :], 0.0)
            v = step(nc.vector.memset(uncovered[:, :, :], 0.0))
            dve.wait_ge(s_own, v)
            nc.vector.memset(pad_row[:, P:P + 1], PAD_SCORE)
            for b in range(TILES):
                nc.vector.memset(uncovered[:, b, SLOTS[b]:KEEP], 1.0)
            nc.vector.memset(rec_out[:, :, KEEP:REC], 0)
            dve.wait_ge(s_iota, 6)
            nc.vector.tensor_scalar(before[:, :], diff[:, :], 0.0, None, ALU.is_gt)
            v = step(nc.vector.tensor_scalar(ident[:, :], diff[:, :], 0.0, None, ALU.is_equal))
            dve.wait_ge(s_own, v)
            nc.vector.tensor_copy(rec_out[:, :, KEEP], target[:, :]).then_inc(s_const, 1)

            def layer_norm(L, g):
                q = made(L, g)
                if L == 0:
                    dve.wait_ge(s_x[g], 16)
                else:
                    dve.wait_ge(s_added, 4 * ((L - 1) * GROUPS + g + 1))
                for t in range(TILES):
                    last = nc.vector.bn_stats(stats[:, t, :], X[:, g * TILES + t, :])
                v = step(last)
                dve.wait_ge(s_own, v)
                if q:
                    dve.wait_ge(s_h, q)
                for t in range(TILES):
                    last = nc.vector.bn_aggr(mean_var[:, t, :], stats[:, t, :])
                last.then_inc(s_var, 1)
                dve.wait_ge(s_std, q + 1)
                v = step(nc.vector.reciprocal(rstd[:, :], std[:, :]))
                dve.wait_ge(s_own, v)
                nc.vector.scalar_tensor_tensor(out=shift[:, :], in0=mean_var[:, :, 0], scalar=-1.0, in1=rstd[:, :],
                                               op0=ALU.mult, op1=ALU.mult).then_inc(s_ln, 1)

            at = {}

            def shorten(t, s):
                b = t % TILES
                cand = found[:, t % 2, :]
                if s == 0:
                    dve.wait_ge(s_found, LOADS * (t + 1))
                    at[0] = step(nc.vector.tensor_tensor(key_a[:, :], seg_base[:, :], cand, ALU.subtract))
                elif s == 1:
                    dve.wait_ge(s_own, at[0])
                    at[1] = step(nc.vector.scalar_tensor_tensor(out=key_b[:, :], in0=cand, scalar=float(SEG),
                                                                in1=key_a[:, :], op0=ALU.is_lt, op1=ALU.mult))
                elif s == 2:
                    dve.wait_ge(s_own, at[1])
                    at[2] = step(nc.vector.max(best[:, b, 0:8], key_b[:, :]))
                elif s == 3:
                    dve.wait_ge(s_own, at[2])
                    at[3] = step(nc.vector.match_replace(key_a[:, :], best[:, b, 0:8], key_b[:, :], 0.0))
                elif s == 4:
                    dve.wait_ge(s_own, at[3])
                    last8 = key_b[:, :].rearrange("p (s k) -> p s k", s=SEGS)[:, :, FOUND - 1]
                    nc.vector.tensor_tensor(full_seg[:, :], full_seg[:, :], last8, ALU.max)
                    at[4] = step(nc.vector.max(best[:, b, 8:16], key_a[:, :]))
                elif s == 5:
                    dve.wait_ge(s_own, at[4])
                    at[5] = step(nc.vector.match_replace(key_b[:, :], best[:, b, 8:16], key_a[:, :], 0.0))
                elif s == 6:
                    dve.wait_ge(s_own, at[5])
                    at[6] = step(nc.vector.max(best[:, b, 16:24], key_b[:, :]))

            def search(t):
                for s in range(SEGS):
                    h = t * LOADS + s // HALF
                    if s % HALF == 0:
                        dve.wait_ge(s_adj[h % RING], 16 * (h // RING + 1))
                    last = nc.vector.max_index(found[:, t % 2, s * FOUND:(s + 1) * FOUND], ones8[:, :],
                                               ring[:, h % RING, s % HALF, :])
                    if s % HALF == HALF - 1:
                        last.then_inc(s_found, 1)
                    if t % TILES:
                        shorten(t - 1, s)
                if t % TILES:
                    for s in range(SEGS, 7):
                        shorten(t - 1, s)

            def sort_rows(g):
                for s in range(7):
                    shorten(g * TILES + TILES - 1, s)
                dve.wait_ge(s_own, at[6])
                v = step(nc.vector.tensor_scalar(cells[:, :, :], best[:, :, :], 0.0, None, ALU.is_gt))
                dve.wait_ge(s_own, v)
                v = step(nc.vector.tensor_reduce(deg[:, :], cells[:, :, :], AX.X, ALU.add))
                dve.wait_ge(s_own, v)
                nc.vector.tensor_tensor(is_class[:, :, :], class_of[:, :, :],
                                        deg[:, :].unsqueeze(1).broadcast_to([P, CLASSES, TILES]),
                                        ALU.is_equal).then_inc(s_class, 1)
                if g:
                    dve.wait_ge(s_rec, 16 * TILES * g)
                nc.vector.tensor_scalar(rec_out[:, :, 0:KEEP], best[:, :, :], -1.0, float(N), ALU.mult, ALU.add)
                dve.wait_ge(s_counts, g + 1)
                cols = CLASSES * TILES
                v = step(nc.vector.tensor_tensor_scan(ahead[:, :], zeros_b[:, 0:cols], WH[1][:, 0:cols], 0.0, ALU.add, ALU.add))
                dve.wait_ge(s_own, v)
                v = step(nc.vector.tensor_tensor(ahead[:, :], ahead[:, :], WH[1][:, 0:cols], ALU.subtract))
                dve.wait_ge(s_own, v)
                v = step(nc.vector.tensor_tensor(ahead[:, :], ahead[:, :], WH[0][:, 0:cols], ALU.add))
                dve.wait_ge(s_own, v)
                v = step(nc.vector.tensor_tensor(picked[:, :, :].rearrange("p d t -> p (d t)"), ahead[:, :],
                                                 is_class[:, :, :].rearrange("p d t -> p (d t)"), ALU.mult))
                dve.wait_ge(s_own, v)
                v = step(nc.vector.tensor_reduce(rank[:, :], picked[:, :, :].rearrange("p d t -> p t d"), AX.X, ALU.add))
                dve.wait_ge(s_own, v)
                v = step(nc.vector.tensor_copy(rank_int[:, :], rank[:, :]))
                dve.wait_ge(s_own, v)
                nc.vector.tensor_scalar(rank_lo[:, :], rank_int[:, :], P - 1, TILES.bit_length() - 1, ALU.bitwise_and,
                                        ALU.logical_shift_left)
                v = step(nc.vector.tensor_scalar(rank_hi[:, :], rank_int[:, :], P.bit_length() - 1, None,
                                                 ALU.logical_shift_right))
                dve.wait_ge(s_own, v)
                v = step(nc.vector.tensor_tensor(rank_at[:, :], rank_lo[:, :], rank_hi[:, :], ALU.bitwise_or))
                dve.wait_ge(s_own, v)
                nc.vector.tensor_scalar(target[:, :], rank_at[:, :], group_base[:, g:g + 1], None,
                                        ALU.add).then_inc(s_target, 1)

            def stage_wide(g):
                nc.vector.tensor_copy(idx_wide[:, :], lists[:, g, 0, 0:WIDE]).then_inc(s_idx_wide, 1)

            def stage_rest(g):
                nc.vector.tensor_copy(idx_rest[:, :, :], lists[:, g, :, 0:NARROW]).then_inc(s_idx_rest, 1)

            def take_lists(g):
                dve.wait_ge(s_lists, 16 * (g + 1))
                stage_wide(g)
                stage_rest(g)
                rows = slice(g * TILES, (g + 1) * TILES)
                nc.vector.tensor_copy(place[:, rows], lists[:, g, :, KEEP])
                nc.vector.tensor_scalar(alone[:, rows], lists[:, g, :, 0], float(N), None, ALU.is_equal)
                v = step(nc.vector.scalar_tensor_tensor(out=cells[:, :, :], in0=lists[:, g, :, 0:KEEP],
                                                        scalar=float(N), in1=uncovered[:, :, :], op0=ALU.is_lt,
                                                        op1=ALU.mult))
                dve.wait_ge(s_own, v)
                nc.vector.tensor_reduce(stair[:, g:g + 1], cells[:, :, :], AX.XY, ALU.max)

            def ways_back(L, g, b):
                n = turn(L, g, b)
                if n >= 2:
                    dve.wait_ge(s_back, n - 1)
                nc.vector.tensor_scalar(Q[:, b % 2, :], iota_group[:, :], place[:, g * TILES + b:g * TILES + b + 1],
                                        None, ALU.is_equal)

            def reduce_max(L, g, b):
                ways_back(L, g, b)
                dve.wait_ge(s_gath[b], 16 * SLOTS[b] * (L * GROUPS + g + 1))
                nc.vector.tensor_reduce(agg[:, b % 2, :], region(b, P).rearrange("p (k f) -> p f k", f=P), AX.X,
                                        ALU.max).then_inc(s_agg, 1)
                next_lists(L, g, b)

            def next_lists(L, g, b):
                if L or g == GROUPS - 1:
                    if L * GROUPS + g + 1 < LAYERS * GROUPS:
                        if b == 0:
                            stage_wide((g + 1) % GROUPS)
                        if b == TILES - 1:
                            stage_rest((g + 1) % GROUPS)

            def add_up(L, g):
                dve.wait_ge(s_back, turn(L, g, TILES))
                for c in range(4):
                    rows = X[:, g * TILES + 4 * c:g * TILES + 4 * c + 4, :].rearrange("p t f -> p (t f)")
                    if L < 3:
                        ins = nc.vector.tensor_tensor(rows, rows, U[c][:, :], ALU.add)
                    else:
                        ins = nc.vector.scalar_tensor_tensor(out=rows, in0=U[c][:, :], scalar=0.0, in1=rows,
                                                             op0=ALU.max, op1=ALU.add)
                    ins.then_inc(s_added, 1)
                if L < 3:
                    layer_norm(L + 1, g)

            for g in range(GROUPS):
                done = 0
                for b in range(TILES):
                    search(g * TILES + b)
                    if g == 0 and b % (TILES // GROUPS) == TILES // GROUPS - 1:
                        layer_norm(0, b // (TILES // GROUPS))
                    if g:
                        if b == 3:
                            take_lists(g - 1)
                        while b > 3 and done < (b - 3) * TILES // (TILES - 4):
                            reduce_max(0, g - 1, done)
                            done += 1
                if g:
                    add_up(0, g - 1)
                sort_rows(g)
            take_lists(GROUPS - 1)
            for b in range(TILES):
                reduce_max(0, GROUPS - 1, b)
            add_up(0, GROUPS - 1)

            dve.wait_ge(s_checked, NT * LOADS)
            nc.vector.tensor_reduce(faults[:, 0:1], full_seg[:, :], AX.X, ALU.max)
            nc.vector.tensor_reduce(faults[:, 1:2], stair[:, :], AX.X, ALU.max)
            v = step(nc.vector.tensor_scalar(odd_sums[:, :], sums[:, :], HALF * SEG / 4, None, ALU.not_equal))
            dve.wait_ge(s_own, v)
            v = step(nc.vector.tensor_reduce(faults[:, 2:3], odd_sums[:, :], AX.X, ALU.max))
            dve.wait_ge(s_own, v)
            nc.vector.tensor_reduce(fault[:, :], faults[:, 0:3], AX.X, ALU.max).then_inc(s_flt, 1)
            places = lists[:, :, :, KEEP].rearrange("p g t -> p (g t)")
            nc.vector.tensor_scalar(place_lo[:, :], places, P - 1, None, ALU.bitwise_and)
            v = step(nc.vector.tensor_scalar(place_hi[:, :], places, P.bit_length() - 1, None, ALU.logical_shift_right))
            dve.wait_ge(s_own, v)
            nc.vector.tensor_copy(in_tile[:, :], place_lo[:, :])
            v = step(nc.vector.tensor_copy(tile_no[:, :], place_hi[:, :]))
            dve.wait_ge(s_own, v)
            nc.vector.tensor_tensor(tile_of[:, :, :], iota_group[:, 0:TILES].unsqueeze(1).broadcast_to([P, NT, TILES]),
                                    tile_no[:, :].unsqueeze(2).broadcast_to([P, NT, TILES]), ALU.is_equal)
            v = step(nc.vector.memset(wh_rows[:, :, P + 2:ROW], 0.0))
            dve.wait_ge(s_fltsum, 1)
            nc.vector.tensor_scalar(flag[:, :], MEAN[:, 0:1], 0.0, None, ALU.is_gt).then_inc(s_flag, 1)

            def scores(L, g, b):
                k, r = SLOTS[b], b % 2
                rows = region(b, ROW).rearrange("p (k f) -> p k f", f=ROW)
                dve.wait_ge(s_gath[b], 16 * k * (L * GROUPS + g + 1))
                v = step(nc.vector.tensor_scalar(score[:, r, 0:k], rows[:, :, P], e1[:, g * TILES + b:g * TILES + b + 1],
                                                 None, ALU.add))
                dve.wait_ge(s_own, v)
                v = step(nc.vector.scalar_tensor_tensor(out=leaky[:, r, 0:k], in0=score[:, r, 0:k], scalar=SLOPE[L],
                                                        in1=score[:, r, 0:k], op0=ALU.mult, op1=ALU.max))
                dve.wait_ge(s_own, v)
                nc.vector.tensor_reduce(neg_max[:, r:r + 1], leaky[:, r, 0:k], AX.X, ALU.max,
                                        negate=True).then_inc(s_scores, 1)

            def weigh(L, g, b):
                k, r, t = SLOTS[b], b % 2, g * TILES + b
                rows = region(b, ROW).rearrange("p (k f) -> p k f", f=ROW)[:, :, 0:P]
                dve.wait_ge(s_prob, turn(L - 2, g, b) + 1)
                v = step(nc.vector.reciprocal(rden[:, r:r + 1], den[:, r:r + 1]))
                ways_back(L, g, b)
                dve.wait_ge(s_own, v)
                v = step(nc.vector.tensor_scalar(weight[:, 0:k], prob[:, r, 0:k], rden[:, r:r + 1], None, ALU.mult))
                dve.wait_ge(s_own, v)
                v = step(nc.vector.tensor_tensor(rows, rows, weight[:, 0:k].unsqueeze(2).broadcast_to([P, k, P]),
                                                 ALU.mult))
                dve.wait_ge(s_own, v)
                v = step(nc.vector.tensor_reduce(num[:, :], rows.rearrange("p k f -> p f k"), AX.X, ALU.add))
                dve.wait_ge(s_own, v)
                nc.vector.scalar_tensor_tensor(out=agg[:, b % 2, :], in0=mean_wh[:, :], scalar=alone[:, t:t + 1],
                                               in1=num[:, :], op0=ALU.mult, op1=ALU.add).then_inc(s_agg, 1)
                next_lists(L, g, b)

            for L in range(1, LAYERS):
                if L >= 2:
                    dve.wait_ge(s_e1, (L - 1) * GROUPS)
                    for half in range((GROUPS + 1) // 2):
                        m = min(2, GROUPS - 2 * half) * TILES
                        rows = slice(2 * half * TILES, 2 * half * TILES + m)
                        v = step(nc.vector.tensor_tensor(
                            e1_pick[:, rows, :], tile_of[:, rows, :],
                            (TR, WH[0])[half][:, 0:m * TILES].rearrange("p (t a) -> p t a", a=TILES), ALU.mult))
                    dve.wait_ge(s_own, v)
                    v = step(nc.vector.tensor_reduce(e1[:, :], e1_pick[:, :, :], AX.X, ALU.add))
                    dve.wait_ge(s_own, v)
                    dve.sem_inc(s_e1used, 1)
                    dve.wait_ge(s_mean, (L - 1) * GROUPS)
                    v = step(nc.vector.tensor_scalar(mean_wh[:, :], MEAN[:, 0:P], 1.0 / N, None, ALU.mult))
                    dve.wait_ge(s_own, v)
                    dve.sem_inc(s_meanused, 1)
                for g in range(GROUPS):
                    for b in range(TILES):
                        if L == 1:
                            reduce_max(L, g, b)
                            if g == 0:
                                for r in range(b * NT // 64, (b + 1) * NT // 64):
                                    if r >= 2:
                                        dve.wait_ge(s_spot_t, r - 1)
                                    for j in range(4):
                                        last = nc.vector.tensor_scalar(
                                            spot[:, 4 * (r % 2) + j, :], iota_group[:, 0:P],
                                            in_tile[:, 4 * r + j:4 * r + j + 1], None, ALU.is_equal)
                                    last.then_inc(s_spot, 1)
                        else:
                            if b == 0:
                                scores(L, g, 0)
                            if b + 1 < TILES:
                                scores(L, g, b + 1)
                            weigh(L, g, b)
                    add_up(L, g)

            dve.wait_ge(s_out, 16 * GROUPS)
            with dve.If(dve.value_load(flag[0:1, 0:1], min_val=0, max_val=1) > 0):
                for s in (d_tile, *d_used):
                    dve.sem_inc(s, 1)
                dve.wait_ge(d_x, 16)
                for L in range(LAYERS):
                    with dve.Fori(0, NT) as t:
                        dve.wait_ge(d_h, t + (L * NT + 1))
                        nc.vector.bn_stats(stats[:, 0, :], X[:, bass.ds(t, 1), :])
                        dve.drain()
                        nc.vector.bn_aggr(mean_var[:, 0, :], stats[:, 0, :]).then_inc(d_var, 1)
                        dve.wait_ge(d_std, t + (L * NT + 1))
                        nc.vector.reciprocal(rstd[:, 0:1], std[:, 0:1])
                        dve.drain()
                        nc.vector.scalar_tensor_tensor(out=shift[:, 0:1], in0=mean_var[:, 0, 0:1], scalar=-1.0,
                                                       in1=rstd[:, 0:1], op0=ALU.mult, op1=ALU.mult).then_inc(d_ln, 1)
                    dve.wait_ge(d_tab, 16 * tab_count(L, NT))
                    if L >= 2:
                        nc.vector.memset(mean_wh[:, 0:1], FILL[L])
                        dve.wait_ge(d_e2, 16 * (L - 1))
                    with dve.Fori(0, NT) as t:
                        dve.wait_ge(d_adj, 16 * t + 16 * (L * NT + 1))
                        if L < 2:
                            nc.vector.tensor_scalar(d_weight, d_edges, 0.0, None, ALU.not_equal)
                        else:
                            nc.vector.tensor_scalar(d_weight, d_target, e1_by_row[:, bass.ds(t, 1)], None, ALU.add)
                            nc.vector.tensor_scalar(d_edges, d_edges, 0.0, None, ALU.is_le)
                            dve.drain()
                            nc.vector.scalar_tensor_tensor(out=d_weight, in0=d_weight, scalar=SLOPE[L], in1=d_weight,
                                                           op0=ALU.mult, op1=ALU.max)
                            dve.drain()
                            nc.vector.copy_predicated(d_weight, d_edges, mean_wh[:, 0:1].broadcast_to([P, N]))
                            dve.drain()
                            nc.vector.tensor_reduce(neg_max[:, 0:1], d_weight, AX.X, ALU.max,
                                                    negate=True).then_inc(d_scores, 1)
                            dve.wait_ge(d_prob, t + ((L - 2) * NT + 1))
                            nc.vector.reciprocal(rden[:, 0:1], den[:, 0:1])
                        nc.vector.memset(num[:, :], 0.0)
                        dve.drain()
                        how = ALU.max if L < 2 else ALU.add
                        with dve.Fori(0, PAIRS) as c:
                            for i in range(2):
                                dve.wait_ge(d_rows[i], 16 * (t * PAIRS + c) + 16 * (L * NT * PAIRS + 1))
                                part = d_weight[:, bass.ds(c * (2 * CHUNK) + i * CHUNK, CHUNK)]
                                nc.vector.tensor_tensor(d_prod, d_chunk[i],
                                                        part.unsqueeze(2).broadcast_to([P, CHUNK, P]),
                                                        ALU.mult).then_inc(d_used[i], 1)
                                dve.drain()
                                nc.vector.tensor_reduce(agg[:, 0, :], d_prod.rearrange("p k f -> p f k"), AX.X, how)
                                dve.drain()
                                nc.vector.tensor_tensor(num[:, :], num[:, :], agg[:, 0, :], how)
                                dve.drain()
                        if L >= 2:
                            nc.vector.tensor_scalar(num[:, :], num[:, :], rden[:, 0:1], 0.0 if L == 3 else None,
                                                    ALU.mult, *([ALU.max] if L == 3 else []))
                            dve.drain()
                        rows = X[:, bass.ds(t, 1), :].rearrange("p t f -> p (t f)")
                        nc.vector.tensor_tensor(rows, rows, num[:, :], ALU.add).then_inc(d_tile, 1)
                    dve.drain()


def kernel(x, adj, L2_gnn_Ws, L2_gnn_a, L3_gnn_W, L3_gnn_a):
    import numpy as _np
    import concourse.bacc as _bacc
    from concourse import mybir as _mybir
    from concourse.bass_utils import run_bass_kernel_spmd as _run

    nc = _bacc.Bacc("TRN2", target_bir_lowering=False, num_devices=1)
    arrays, args = {}, []
    for name, a in (("x", x), ("adj", adj), ("w2", L2_gnn_Ws), ("a2", L2_gnn_a), ("w3", L3_gnn_W), ("a3", L3_gnn_a)):
        a = _np.ascontiguousarray(a)
        arrays[f"in_{name}"] = a
        args.append(nc.dram_tensor(f"in_{name}", a.shape, _mybir.dt.from_np(a.dtype), kind="ExternalInput").ap())
    args.append(nc.dram_tensor("out_h", tuple(x.shape), _mybir.dt.float32, kind="ExternalOutput").ap())
    gnn_kernel(nc, *args)
    return _run(nc, [arrays], core_ids=[0]).results[0]["out_h"]
```

```python
import concourse.bass as bass
from concourse import mybir
from contextlib import ExitStack

P = 128
TILES = 16
SEG = 1024
FOUND = 8
KEEP = 24
REC = 28
HALF = 4
RING = 4
ROW = 132

SLOTS = [20, 8, 7, 6, 5, 5, 5, 4, 4, 4, 3, 3, 3, 2, 2, 1]
DEEP_FROM = {0: 14, 1: 7, 2: 6}
DEEP_SLOTS = sum(SLOTS[b] - k for b, k in DEEP_FROM.items())
ORDER = [13, 14, 15, 10, 11, 12, 0, 1, 2, 3, 4, 5, 6, 9, 8, 7]
AT = [sum(SLOTS[:b]) for b in range(TILES)]
SLOTS_ALL = sum(SLOTS)
QUARTER = TILES // 4
WAYS_BY_ACT = [6, 8, 10, 12, 14]
AHEAD = 4

LN_EPS = 1e-5
SLOPE = {2: 0.2, 3: 0.01}
FILL = {2: -9000000000000000.0, 3: -9e16}
PAD_SCORE = -1e30


def gnn_kernel(nc, x, adj, w2, a2, w3, a3, out):
    f32, i32, u32, bf16 = mybir.dt.float32, mybir.dt.int32, mybir.dt.uint32, mybir.dt.bfloat16
    f16 = mybir.dt.float16
    ALU, ACT, AX = mybir.AluOpType, mybir.ActivationFunctionType, mybir.AxisListType

    N = x.shape[0]
    GROUPS = N // (P * TILES)
    NT = N // P
    GROUP = P * TILES
    SEGS = N // SEG
    LOADS = SEGS // HALF
    CAND = SEGS * FOUND
    LAYERS = 4
    CLASSES = KEEP + 1

    tab = [nc.dram_tensor(f"table_{n}", (N + 1, P if n < 2 else ROW), f32, kind="Internal").ap() for n in range(LAYERS)]
    scores_dram = nc.dram_tensor("scores_dram", (N,), f32, kind="Internal").ap()
    records = nc.dram_tensor("records", (N, REC), u32, kind="Internal").ap()

    ctx = ExitStack()
    with ctx:
        def sb(name, shape, dt):
            return ctx.enter_context(nc.sbuf_tensor(name, shape, dt))

        def pb(name, shape, dt):
            return ctx.enter_context(nc.psum_tensor(name, shape, dt))

        def sem(name):
            return ctx.enter_context(nc.semaphore(name))

        arena = sb("arena", [P, RING * HALF * (SEG + FOUND)], i32)
        ring = arena[:, :].rearrange("p (r s c) -> p r s c", r=RING, s=HALF)
        after = arena[:, :].bitcast(f32)
        place_t = after[:, 0:NT * P].rearrange("p (t i) -> p t i", t=NT)
        o = NT * P
        wh_rows = after[:, o:o + TILES * ROW].rearrange("p (t f) -> p t f", t=TILES)
        o += TILES * ROW
        h_t = after[:, o:o + 4 * P]
        o += 4 * P
        tile_of = after[:, o:o + NT * TILES].rearrange("p (t a) -> p t a", t=NT)
        o += NT * TILES
        e1_pick = after[:, o:o + NT * TILES].rearrange("p (t a) -> p t a", t=NT)
        o += NT * TILES
        spot = after[:, o:o + 8 * P].rearrange("p (k i) -> p k i", k=8)
        o += 8 * P

        checked_out = sb("checked_out", [P, HALF, SEG], mybir.dt.uint8)
        X = sb("X", [P, NT, P], f32)
        G = sb("G", [P, SLOTS_ALL * ROW], f32)
        H = sb("H", [P, TILES, P], f32)
        Q = sb("Q", [P, AHEAD, GROUP], bf16)
        lists = sb("lists", [P, GROUPS, TILES, REC], u32)
        agg = sb("agg", [P, 2, P], f32)
        rest = sb("rest", [P, 2, P], f32)
        parts = sb("parts", [P, AHEAD, 3, P], bf16)
        places_row = sb("places_row", [P, GROUP], f16)

        found = sb("found", [P, 2, CAND], u32)
        key_a = sb("key_a", [P, CAND], f32)
        key_b = sb("key_b", [P, CAND], f32)
        seg_base = sb("seg_base", [P, CAND], f32)
        ones8 = sb("ones8", [P, FOUND], f32)
        best = sb("best", [P, TILES, KEEP], f32)
        uncovered = sb("uncovered", [P, TILES, KEEP], bf16)
        full_seg = sb("full_seg", [P, SEGS], f32)
        deg = sb("deg", [P, TILES], f32)
        class_of = sb("class_of", [P, CLASSES, TILES], bf16)
        is_class = sb("is_class", [P, CLASSES, TILES], bf16)
        ahead = sb("ahead", [P, CLASSES * TILES], f32)
        picked = sb("picked", [P, CLASSES, TILES], f32)
        cells = picked[:, :, :].rearrange("p d t -> p (d t)")[:, 0:TILES * KEEP].rearrange("p (t k) -> p t k", t=TILES)
        rank = sb("rank", [P, TILES], f32)
        rank_int = sb("rank_int", [P, TILES], u32)
        rank_hi = sb("rank_hi", [P, TILES], u32)
        rank_lo = sb("rank_lo", [P, TILES], u32)
        rank_at = sb("rank_at", [P, TILES], u32)
        target = sb("target", [P, TILES], u32)
        group_base = sb("group_base", [P, GROUPS], f32)
        rec_out = sb("rec_out", [P, TILES, REC], u32)
        place = sb("place", [P, NT], f32)
        alone = sb("alone", [P, NT], f32)
        in_tile = sb("in_tile", [P, NT], f32)
        tile_no = sb("tile_no", [P, NT], f32)
        place_lo = sb("place_lo", [P, NT], u32)
        place_hi = sb("place_hi", [P, NT], u32)

        stats = sb("stats", [P, TILES, 6], f32)
        mean_var = sb("mean_var", [P, TILES, 2], f32)
        std = sb("std", [P, TILES], f32)
        rstd = sb("rstd", [P, TILES], f32)
        shift = sb("shift", [P, TILES], f32)
        eps = sb("eps", [P, 1], f32)
        minus_half = sb("minus_half", [P, 1], f32)

        scores = sb("scores", [P, 2, SLOTS[0]], f32)
        leaky = sb("leaky", [P, 2, SLOTS[0]], f32)
        prob = sb("prob", [P, 2, SLOTS[0]], f32)
        neg_max = sb("neg_max", [P, 2], f32)
        den = sb("den", [P, 2], f32)
        rden = sb("rden", [P, 2], f32)
        num = sb("num", [P, 2, P], f32)
        mean_wh = sb("mean_wh", [P, P], f32)
        e1_by_row = sb("e1_by_row", [P, NT], f32)
        e1 = sb("e1", [P, NT], f32)

        sums = sb("sums", [P, NT * LOADS], f32)
        odd_sums = sb("odd_sums", [P, NT * LOADS], f32)
        stair = sb("stair", [P, GROUPS], f32)
        faults = sb("faults", [P, 3], f32)
        fault = sb("fault", [P, 1 + GROUPS], f32)
        flag = sb("flag", [P, 1 + GROUPS], i32)
        least_in = sb("least_in", [P, GROUPS], f32)
        least_two = sb("least_two", [P, GROUPS], f32)
        last_in = sb("last_in", [P, GROUPS, len(DEEP_FROM)], f32)

        diff = sb("diff", [P, P], f32)
        ident = sb("ident", [P, P], f32)
        before = sb("before", [P, P], bf16)
        ones_b = sb("ones_b", [P, P], bf16)
        ones_f = sb("ones_f", [P, P], f32)
        zeros_b = sb("zeros_b", [P, 512], bf16)
        pad_row = sb("pad_row", [1, ROW], f32)
        pad_zero = sb("pad_zero", [1, P], f32)
        w_in = {L: sb(f"w_in{L}", [P, P], f32) for L in (2, 3)}
        w_t2 = sb("w_t2", [P, P], f32)
        w_aug = {L: sb(f"w_aug{L}", [P, P + 2], f32) for L in (2, 3)}
        a_cols = {L: sb(f"a_cols{L}", [P, 2], f32) for L in (2, 3)}

        U = [pb(f"U{c}", [P, 512], f32) for c in range(4)]
        TR = pb("TR", [P, 512], f32)
        WH = [pb(f"WH{c}", [P, 512], f32) for c in range(2)]
        MEAN = pb("MEAN", [P, 512], f32)

        s_x = [sem(f"s_x{g}") for g in range(GROUPS)]
        s_w = sem("s_w")
        s_iota = sem("s_iota")
        s_const = sem("s_const")
        s_pads = sem("s_pads")
        s_own = sem("s_own")
        s_adj = [sem(f"s_adj{r}") for r in range(RING)]
        s_found = sem("s_found")
        s_checked = sem("s_checked")
        s_class = sem("s_class")
        s_counts = sem("s_counts")
        s_target = sem("s_target")
        s_rec = sem("s_rec")
        s_lists = sem("s_lists")
        s_deep_rows = [sem(f"s_deep_rows{g}") for g in range(GROUPS)]
        s_deep = sem("s_deep")
        s_blank = sem("s_blank")
        s_gath = [sem(f"s_gath{b}") for b in range(TILES)]
        s_agg = sem("s_agg")
        s_back = sem("s_back")
        s_bank = sem("s_bank")
        s_ways = sem("s_ways")
        s_added = sem("s_added")
        s_var = sem("s_var")
        s_std = sem("s_std")
        s_ln = sem("s_ln")
        s_h = sem("s_h")
        s_hn = sem("s_hn")
        s_tab = [sem(f"s_tab{n}") for n in range(LAYERS)]
        s_tr = sem("s_tr")
        s_ht = sem("s_ht")
        s_wh = sem("s_wh")
        s_wt = sem("s_wt")
        s_e1r = sem("s_e1r")
        s_mean = sem("s_mean")
        s_meanused = sem("s_meanused")
        s_e1 = sem("s_e1")
        s_e1used = sem("s_e1used")
        s_spot = sem("s_spot")
        s_spot_t = sem("s_spot_t")
        s_place_t = sem("s_place_t")
        s_scores = sem("s_scores")
        s_prob = sem("s_prob")
        s_wprep = sem("s_wprep")
        s_wcopy = sem("s_wcopy")
        s_flt = sem("s_flt")
        s_fltsum = sem("s_fltsum")
        s_flag = sem("s_flag")
        s_out = sem("s_out")

        d_x = sem("d_x")
        d_var = sem("d_var")
        d_std = sem("d_std")
        d_ln = sem("d_ln")
        d_h = sem("d_h")
        d_pe = sem("d_pe")
        d_cp = sem("d_cp")
        d_tab = sem("d_tab")
        d_e2 = sem("d_e2")
        d_adj = sem("d_adj")
        d_scores = sem("d_scores")
        d_prob = sem("d_prob")
        d_rows = [sem(f"d_rows{i}") for i in range(2)]
        d_used = [sem(f"d_used{i}") for i in range(2)]
        d_tile = sem("d_tile")
        d_out = sem("d_out")

        block = ctx.enter_context(nc.Block())

        d_edges = arena[:, 0:N]
        d_target = after[:, N:2 * N]
        d_weight = G[:, 0:N]
        d_pair = Q[:, :, :].rearrange("p k i -> p (k i)").bitcast(f32).rearrange("p (k f) -> p k f", f=P)
        d_chunk = [H[:, :, :], d_pair[:, TILES:2 * TILES, :]]
        d_prod = d_pair[:, 0:TILES, :]
        CHUNK = TILES
        PAIRS = N // (2 * CHUNK)

        def tab_count(L, t):
            return (L * NT + t) if L < 2 else (2 * NT + 2 * ((L - 2) * NT + t))

        def region(b):
            return G[:, AT[b] * ROW:(AT[b] + SLOTS[b]) * ROW].rearrange("p (k f) -> p k f", f=ROW)

        def some_deep(L, g):
            return L * GROUPS + g >= GROUPS - 1

        def slots_of(L, g, b):
            return DEEP_FROM.get(b, SLOTS[b]) if some_deep(L, g) else SLOTS[b]

        def turn(L, g, j):
            return (L * GROUPS + g) * TILES + j

        def ways_by_act(L, j):
            return L >= 2 and j in WAYS_BY_ACT

        def ways_made(L, g, j):
            return 2 * (((L - 2) * GROUPS + g) * len(WAYS_BY_ACT) + WAYS_BY_ACT.index(j) + 1)

        def between_attention(L, g):
            return L == 3 and g < GROUPS - 1

        def reduced_after(t):
            return min(TILES, max(0, (t - 4) * TILES // 8))

        def left_by_sync(L, g):
            return L >= 2 or (L == 1 and g >= GROUPS - 2)

        def made(L, g):
            return L * GROUPS + g

        @block.sync
        def _(sp):
            for h in range(NT * LOADS):
                g = h // (TILES * LOADS // GROUPS)
                if h % (TILES * LOADS // GROUPS) == RING and g < GROUPS:
                    sp.dma_start(X[:, g * TILES:(g + 1) * TILES, :],
                                 x[g * GROUP:(g + 1) * GROUP, :].rearrange("(t p) f -> p t f", p=P)
                                 ).then_inc(s_x[g], 16)
                if h >= RING:
                    sp.wait_ge(s_found, h - RING + 1)
                    sp.wait_ge(s_checked, h - RING + 1)
                t, part = h // LOADS, h % LOADS
                src = adj[t * P:(t + 1) * P, part * HALF * SEG:(part + 1) * HALF * SEG]
                sp.dma_start(ring[:, h % RING, :, 0:SEG],
                             src.rearrange("p (s c) -> p s c", s=HALF)).then_inc(s_adj[h % RING], 16)
            for L in range(1, LAYERS):
                for g in range(GROUPS):
                    for c in range(4 if left_by_sync(L, g) else 0):
                        if L == 1:
                            sp.wait_ge(s_h, 4 * made(L, g) + c + 1)
                        else:
                            sp.wait_ge(s_wt, 2 * (4 * ((L - 2) * GROUPS + g) + c) + 2)
                        t = g * TILES + c * QUARTER
                        sp.dma_start(tab[L][t * P:(t + QUARTER) * P, :].rearrange("(t p) f -> p t f", p=P),
                                     (H if L == 1 else wh_rows)[:, c * QUARTER:(c + 1) * QUARTER, :]
                                     ).then_inc(s_tab[L], 16)
            for g in range(GROUPS):
                for c in range(4):
                    sp.wait_ge(s_added, 4 * (3 * GROUPS + g) + c + 1)
                    t = g * TILES + c * QUARTER
                    sp.dma_start(out[t * P:(t + QUARTER) * P, :].rearrange("(t p) f -> p t f", p=P),
                                 X[:, t:t + QUARTER, :]).then_inc(s_out, 16)
            sp.wait_ge(s_out, 64 * GROUPS)

            with sp.If(sp.value_load(flag[0:1, 0:1], min_val=0, max_val=1) > 0):
                sp.dma_start(X[:, :, :], x.rearrange("(t p) f -> p t f", p=P)).then_inc(d_x, 16)
                for L in range(LAYERS):
                    sp.wait_ge(d_tab, 16 * tab_count(L, NT))
                    if L >= 2:
                        sp.dma_start(d_target, scores_dram.rearrange("(o n) -> o n", o=1).broadcast_to([P, N])
                                     ).then_inc(d_e2, 16)
                    with sp.Fori(0, NT) as t:
                        sp.wait_ge(d_tile, t + (L * NT + 1))
                        sp.dma_start(d_edges, adj[bass.ds(t * P, P), :]).then_inc(d_adj, 16)
                        with sp.Fori(0, PAIRS) as c:
                            for i in range(2):
                                sp.wait_ge(d_used[i], t * PAIRS + c + (L * NT * PAIRS + 1))
                                rows = tab[L][bass.ds(c * (2 * CHUNK) + i * CHUNK, CHUNK), 0:P]
                                sp.dma_start(d_chunk[i], rows.unsqueeze(0).broadcast_to([P, CHUNK, P])
                                             ).then_inc(d_rows[i], 16)
                sp.wait_ge(d_tile, LAYERS * NT + 1)
                sp.dma_start(out.rearrange("(t p) f -> p t f", p=P), X[:, :, :]).then_inc(d_out, 16)
                sp.wait_ge(d_out, 16)

        @block.gpsimd
        def _(pool):
            nc.gpsimd.iota(H[:, :, :], [[1, GROUP]], base=0, channel_multiplier=0,
                           allow_small_or_imprecise_dtypes=True).then_inc(s_iota, 1)
            nc.gpsimd.iota(seg_base[:, :].rearrange("p (s k) -> p s k", s=SEGS), [[-SEG, SEGS], [0, FOUND]], base=N,
                           channel_multiplier=0, allow_small_or_imprecise_dtypes=True).then_inc(s_iota, 1)
            nc.gpsimd.iota(class_of[:, :, :], [[-1, CLASSES], [0, TILES]], base=KEEP, channel_multiplier=0,
                           allow_small_or_imprecise_dtypes=True).then_inc(s_iota, 1)
            nc.gpsimd.iota(group_base[:, :], [[GROUP, GROUPS]], base=0, channel_multiplier=0,
                           allow_small_or_imprecise_dtypes=True).then_inc(s_iota, 1)
            nc.gpsimd.iota(diff[:, :], [[1, P]], base=0, channel_multiplier=-1,
                           allow_small_or_imprecise_dtypes=True).then_inc(s_iota, 1)
            nc.gpsimd.iota(target[:, :], [[P, TILES]], base=0, channel_multiplier=1).then_inc(s_iota, 1)

            def gather_slots(L, g, b, slots, done):
                width = P if L < 2 else ROW
                for k in slots:
                    pool.indirect_dma_start(region(b)[:, k, 0:width], None, tab[L],
                                            bass.IndirectOffsetOnAxis(ap=lists[:, g, b, k:k + 1], axis=0),
                                            bounds_check=N, oob_is_err=False).then_inc(done, 16)

            deep = []

            def gather(L, g):
                for j, b in enumerate(ORDER):
                    if turn(L, g, j) >= TILES:
                        pool.wait_ge(s_agg, turn(L, g, j) - TILES + 1)
                    if some_deep(L, g) and turn(L, g, j) == turn(0, GROUPS - 1, 0):
                        pool.wait_ge(s_blank, 1)
                    gather_slots(L, g, b, range(slots_of(L, g, b)), s_gath[b])
                    if b == max(DEEP_FROM) and some_deep(L, g):
                        if not deep:
                            pool.wait_ge(s_flag, 1)
                            deep.extend(pool.value_load(flag[0:1, 1 + i:2 + i], min_val=0, max_val=1)
                                        for i in range(GROUPS))
                        with pool.If(deep[g] > 0):
                            for d, k in DEEP_FROM.items():
                                gather_slots(L, g, d, range(k, SLOTS[d]), s_deep_rows[g])
                            pool.wait_ge(s_deep_rows[g], 16 * DEEP_SLOTS * (L + 1 if some_deep(0, g) else L))
                        pool.sem_inc(s_deep, 1)

            def scatter_lists(g):
                pool.wait_ge(s_target, g + 1)
                for b in range(TILES):
                    pool.indirect_dma_start(records, bass.IndirectOffsetOnAxis(ap=target[:, b:b + 1], axis=0),
                                            rec_out[:, b, :], None, bounds_check=N - 1,
                                            oob_is_err=False).then_inc(s_rec, 16)
                pool.wait_ge(s_rec, 16 * TILES * (g + 1))
                pool.dma_start(lists[:, g, :, :].rearrange("p t r -> p (t r)"),
                               records[g * GROUP:(g + 1) * GROUP, :].rearrange("(p t) r -> p (t r)", p=P)
                               ).then_inc(s_lists, 16)

            for g in range(GROUPS):
                scatter_lists(g)
                if g == 0:
                    pool.wait_ge(s_pads, 16 * LAYERS)
                    pool.wait_ge(s_tab[0], 64 * GROUPS)
                pool.wait_ge(s_lists, 16 * (g + 1))
                gather(0, g)
            for L in range(1, LAYERS):
                pool.wait_ge(s_tab[L], 64 * GROUPS)
                for g in range(GROUPS):
                    gather(L, g)

        @block.scalar
        def _(act):
            act.dma_start(w_in[2][:, :], w2).then_inc(s_w, 16)
            act.dma_start(w_aug[2][:, 0:P], w2).then_inc(s_w, 16)
            act.dma_start(w_in[3][:, :], w3).then_inc(s_w, 16)
            for L, a in ((2, a2), (3, a3)):
                act.dma_start(a_cols[L][:, 0:1], a[P:2 * P, :]).then_inc(s_w, 16)
                act.dma_start(a_cols[L][:, 1:2], a[0:P, :]).then_inc(s_w, 16)
            act.wait_ge(s_const, 1)
            for L in range(LAYERS):
                act.dma_start(tab[L][N:N + 1, :], pad_zero[0:1, :] if L < 2 else pad_row[0:1, :]).then_inc(s_pads, 16)

            def check(h):
                act.wait_ge(s_adj[h % RING], 16 * (h // RING + 1))
                if h:
                    act.wait_ge(s_checked, h)
                nc.scalar.activation(checked_out[:, :, :], ring[:, h % RING, :, 0:SEG], ACT.Square,
                                     bias=minus_half[:, 0:1], accum_out=sums[:, h:h + 1]).then_inc(s_checked, 1)

            def leave(L, g, c, rows):
                if left_by_sync(L, g):
                    return
                t = g * TILES + c * QUARTER
                act.dma_start(tab[L][t * P:(t + QUARTER) * P, :].rearrange("(t p) f -> p t f", p=P),
                              rows[:, c * QUARTER:(c + 1) * QUARTER, :]).then_inc(s_tab[L], 16)

            def deviation(q, c):
                act.wait_ge(s_var, 4 * q + c + 1)
                part = slice(c * QUARTER, (c + 1) * QUARTER)
                nc.scalar.activation(std[:, part], mean_var[:, part, 1], ACT.Sqrt, bias=eps[:, 0:1]).then_inc(s_std, 1)

            def rows_of_max(L, g, c):
                q = made(L, g)
                if c == 0 and q:
                    act.wait_ge(s_tab[(q - 1) // GROUPS], 64 * ((q - 1) % GROUPS + 1))
                act.wait_ge(s_ln, 4 * q + c + 1)
                for t in range(c * QUARTER, (c + 1) * QUARTER):
                    last = nc.scalar.activation(H[:, t, :], X[:, g * TILES + t, :], ACT.Relu,
                                                bias=shift[:, t:t + 1], scale=rstd[:, t:t + 1])
                last.then_inc(s_h, 1)
                act.wait_ge(s_h, 4 * q + c + 1)
                leave(L, g, c, H)

            def rows_of_attention(L, g, c):
                m = 4 * ((L - 2) * GROUPS + g) + c
                act.wait_ge(s_tr, m + 1)
                if m:
                    act.wait_ge(s_wh, 2 * m)
                nc.scalar.activation(h_t[:, :], TR[:, :], ACT.Relu).then_inc(s_ht, 1)
                if c == 0 and m:
                    act.wait_ge(s_tab[2 + (m // 4 - 1) // GROUPS], 64 * ((m // 4 - 1) % GROUPS + 1))
                    act.wait_ge(s_mean, m)
                    act.wait_ge(s_e1r, m)
                for half in range(2):
                    act.wait_ge(s_wh, 2 * m + half + 1)
                    src = WH[half][:, 0:2 * ROW].rearrange("p (t f) -> p t f", t=2)[:, :, 0:P + 2]
                    t = c * QUARTER + 2 * half
                    nc.scalar.copy(wh_rows[:, t:t + 2, 0:P + 2], src).then_inc(s_wt, 1)
                act.wait_ge(s_wt, 2 * m + 2)
                leave(L, g, c, wh_rows)
                if c == 0 and g == 0 and L == 3:
                    act.wait_ge(s_e1, GROUPS)
                t = g * TILES + c * QUARTER
                nc.scalar.copy(e1_by_row[:, t:t + QUARTER],
                               wh_rows[:, c * QUARTER:(c + 1) * QUARTER, P + 1]).then_inc(s_e1r, 1)

            def table_rows(L, g):
                rows = rows_of_max if L < 2 else rows_of_attention
                if between_attention(L, g):
                    for c in range(4):
                        deviation(made(L, g), c)
                    exponentials(L - 1, g + 1, 0)
                    for c in range(4):
                        if c >= 2:
                            exponentials(L - 1, g + 1, c - 1)
                        rows(L, g, c)
                    return
                for c in range(4):
                    deviation(made(L, g), c)
                    if c:
                        rows(L, g, c - 1)
                rows(L, g, 3)

            def half_of_ways(L, g, j, s):
                at = g * TILES + ORDER[j]
                if s == 0:
                    n = turn(L, g, j) - AHEAD
                    act.wait_ge(s_back, n // TILES * (TILES - 1) + n % TILES + 1)
                    nc.scalar.activation(Q[:, j % AHEAD, :], places_row[:, :], ACT.Abs, bias=place[:, at:at + 1],
                                         scale=-1.0).then_inc(s_ways, 1)
                else:
                    act.wait_ge(s_ways, ways_made(L, g, j) - 1)
                    nc.scalar.activation(Q[:, j % AHEAD, :], Q[:, j % AHEAD, :], ACT.Relu, bias=ones_f[:, 0:1],
                                         scale=-1.0).then_inc(s_ways, 1)

            def exponentials(L, g, j):
                act.wait_ge(s_scores, turn(L - 2, g, j) + 1)
                k, r = SLOTS[ORDER[j]], j % 2
                nc.scalar.activation(prob[:, r, 0:k], leaky[:, r, 0:k], ACT.Exp, bias=neg_max[:, r:r + 1],
                                     accum_out=den[:, r:r + 1]).then_inc(s_prob, 1)

            def weights():
                act.wait_ge(s_wprep, 1)
                nc.scalar.copy(w_t2[:, :], TR[:, 0:P])
                nc.scalar.copy(w_aug[3][:, 0:P], TR[:, P:2 * P]).then_inc(s_wcopy, 1)
                act.wait_ge(s_wprep, 2)
                nc.scalar.copy(w_aug[2][:, P:P + 2], WH[0][:, 0:2])
                nc.scalar.copy(w_aug[3][:, P:P + 2], WH[0][:, 2:4]).then_inc(s_wcopy, 1)

            for g in range(GROUPS):
                for t in range(TILES):
                    for part in range(LOADS):
                        check((g * TILES + t) * LOADS + part)
                    if g == 0 and t % (TILES // GROUPS) == TILES // GROUPS - 1:
                        table_rows(0, t // (TILES // GROUPS))
                    if g >= 2 and t == 0:
                        table_rows(1, g - 2)
                    if g == 0 and t == 2:
                        weights()
            table_rows(1, GROUPS - 2)
            table_rows(1, GROUPS - 1)
            for L in range(1, LAYERS):
                for g in range(GROUPS):
                    early = between_attention(L + 1, g - 1) if g else False
                    if L >= 2 and not early:
                        exponentials(L, g, 0)
                    for j in range(TILES):
                        if L >= 2 and j + 1 < TILES and not (early and j < 2):
                            exponentials(L, g, j + 1)
                        for s in range(2):
                            if j + 2 - s < TILES and ways_by_act(L, j + 2 - s) and L >= 2:
                                half_of_ways(L, g, j + 2 - s, s)
                        if L == 1 and g == 0:
                            for r in range(j * NT // 64, (j + 1) * NT // 64):
                                act.wait_ge(s_spot_t, r + 1)
                                nc.scalar.copy(place_t[:, 4 * r:4 * r + 4, :].rearrange("p t i -> p (t i)"),
                                               TR[:, :]).then_inc(s_place_t, 1)
                    if L < 3:
                        table_rows(L + 1, g)

            act.wait_ge(s_out, 64 * GROUPS)
            with act.If(act.value_load(flag[0:1, 0:1], min_val=0, max_val=1) > 0):
                act.sem_inc(d_h, 1)
                for L in range(LAYERS):
                    with act.Fori(0, NT) as t:
                        act.wait_ge(d_var, t + (L * NT + 1))
                        nc.scalar.activation(std[:, 0:1], mean_var[:, 0, 1:2], ACT.Sqrt,
                                             bias=eps[:, 0:1]).then_inc(d_std, 1)
                        act.wait_ge(d_ln, t + (L * NT + 1))
                        nc.scalar.activation(H[:, 0, :], X[:, bass.ds(t, 1), :].rearrange("p t f -> p (t f)"), ACT.Relu,
                                             bias=shift[:, 0:1], scale=rstd[:, 0:1]).then_inc(d_h, 1)
                        act.wait_ge(d_h, t + (L * NT + 2))
                        if L < 2:
                            act.dma_start(tab[L][bass.ds(t * P, P), :], H[:, 0, :]).then_inc(d_tab, 16)
                            act.wait_ge(d_tab, 16 * t + 16 * (tab_count(L, 0) + 1))
                        else:
                            m = (L - 2) * NT
                            act.wait_ge(d_pe, 2 * t + (2 * m + 1))
                            nc.scalar.copy(h_t[:, 0:P], TR[:, 0:P]).then_inc(d_cp, 1)
                            act.wait_ge(d_pe, 2 * t + (2 * m + 2))
                            nc.scalar.copy(e1_by_row[:, bass.ds(t, 1)], WH[0][:, P + 1:P + 2])
                            nc.scalar.copy(wh_rows[:, 0, 0:P + 2], WH[0][:, 0:P + 2]).then_inc(d_cp, 1)
                            act.wait_ge(d_cp, 2 * t + (2 * m + 2))
                            act.dma_start(tab[L][bass.ds(t * P, P), 0:P + 2], wh_rows[:, 0, 0:P + 2]).then_inc(d_tab, 16)
                            act.dma_start(scores_dram[bass.ds(t * P, P)].unsqueeze(1), wh_rows[:, 0, P:P + 1]
                                          ).then_inc(d_tab, 16)
                            act.wait_ge(d_tab, 32 * t + 16 * (tab_count(L, 0) + 2))
                    if L >= 2:
                        with act.Fori(0, NT) as t:
                            act.wait_ge(d_scores, t + ((L - 2) * NT + 1))
                            nc.scalar.activation(d_weight, d_weight, ACT.Exp, bias=neg_max[:, 0:1],
                                                 accum_out=den[:, 0:1]).then_inc(d_prob, 1)

        @block.tensor
        def _(pe):
            pe.wait_ge(s_w, 16 * 7)
            pe.wait_ge(s_const, 1)
            nc.tensor.transpose(TR[:, 0:P], w_in[2][:, :], ident[:, :])
            nc.tensor.transpose(TR[:, P:2 * P], w_in[3][:, :], ident[:, :]).then_inc(s_wprep, 1)
            pe.wait_ge(s_wcopy, 1)
            nc.tensor.matmul(WH[0][:, 0:2], w_t2[:, :], a_cols[2][:, :], start=True, stop=True)
            nc.tensor.matmul(WH[0][:, 2:4], w_in[3][:, :], a_cols[3][:, :], start=True, stop=True).then_inc(s_wprep, 1)
            pe.wait_ge(s_wcopy, 2)

            def rank_counts(g):
                pe.wait_ge(s_class, g + 1)
                oh = is_class[:, :, :].rearrange("p d t -> p (d t)")
                nc.tensor.matmul(WH[0][:, 0:CLASSES * TILES], before[:, :], oh, start=True, stop=True)
                nc.tensor.matmul(WH[1][:, 0:CLASSES * TILES], ones_b[:, :], oh, start=True,
                                 stop=True).then_inc(s_counts, 1)

            def put_back(L, g, j):
                n = turn(L, g, j)
                if j == 0:
                    if n:
                        pe.wait_ge(s_added, 4 * (L * GROUPS + g))
                    for c in range(4):
                        nc.tensor.matmul(U[c][:, :], zeros_b[:, 0:P], zeros_b[:, :], start=True, stop=False,
                                         skip_group_check=True)
                pe.wait_ge(s_agg, n + 1)
                if ways_by_act(L, j):
                    pe.wait_ge(s_ways, ways_made(L, g, j))
                for a in range(TILES):
                    for i in range(3):
                        last = nc.tensor.matmul(U[a // 4][:, (a % 4) * P:(a % 4 + 1) * P],
                                                Q[:, j % AHEAD, a * P:(a + 1) * P], parts[:, j % AHEAD, i, :],
                                                start=False, stop=(j == TILES - 1 and i == 2), skip_group_check=True)
                    if j == TILES - 1 and a % 4 == 3:
                        last.then_inc(s_bank, 1)
                if j < TILES - 1:
                    last.then_inc(s_back, 1)

            def into_mean(L, g, c):
                m = 4 * ((L - 2) * GROUPS + g) + c
                pe.wait_ge(s_wt, 2 * m + 2)
                if c == 0 and g == 0 and L == 3:
                    pe.wait_ge(s_meanused, 1)
                for t in range(c * QUARTER, (c + 1) * QUARTER):
                    last = nc.tensor.matmul(MEAN[:, 0:P], ones_f[:, :], wh_rows[:, t, 0:P],
                                            start=(g == 0 and t == 0), stop=(g == GROUPS - 1 and t == TILES - 1))
                last.then_inc(s_mean, 1)

            def project(L, g):
                for c in range(4):
                    m = 4 * ((L - 2) * GROUPS + g) + c
                    pe.wait_ge(s_hn, m + 1)
                    if m == 0:
                        pe.wait_ge(s_place_t, NT // 4)
                    if c == 0 and m:
                        pe.wait_ge(s_e1used, (L - 2) * GROUPS + g)
                    if m:
                        pe.wait_ge(s_ht, m)
                    for j in range(4):
                        last = nc.tensor.transpose(TR[:, j * P:(j + 1) * P], H[:, 4 * c + j, :], ident[:, :])
                    last.then_inc(s_tr, 1)
                    if c:
                        into_mean(L, g, c - 1)
                    pe.wait_ge(s_ht, m + 1)
                    for half in range(2):
                        if m:
                            pe.wait_ge(s_wt, 2 * m + half - 1)
                        for j in range(2):
                            last = nc.tensor.matmul(WH[half][:, j * ROW:j * ROW + P + 2],
                                                    h_t[:, (2 * half + j) * P:(2 * half + j + 1) * P],
                                                    w_aug[L][:, :], start=True, stop=True)
                        last.then_inc(s_wh, 1)
                if not between_attention(L, g):
                    source_scores(L, g)

            def source_scores(L, g):
                into_mean(L, g, 3)
                pe.wait_ge(s_e1r, 4 * ((L - 2) * GROUPS + g + 1))
                for b in range(TILES):
                    last = nc.tensor.matmul(TR[:, b * TILES:(b + 1) * TILES], place_t[:, g * TILES + b, :],
                                            e1_by_row[:, g * TILES:(g + 1) * TILES], start=True, stop=True)
                last.then_inc(s_e1, 1)

            for g in range(GROUPS):
                if g:
                    for j in range(TILES):
                        put_back(0, g - 1, j)
                rank_counts(g)
            pe.wait_ge(s_flt, 1)
            nc.tensor.matmul(MEAN[:, 0:1 + GROUPS], ones_f[:, :], fault[:, :], start=True, stop=True).then_inc(s_fltsum, 1)
            for j in range(TILES):
                put_back(0, GROUPS - 1, j)
            for L in range(1, LAYERS):
                for g in range(GROUPS):
                    for j in range(TILES):
                        put_back(L, g, j)
                        if j == 2 and g and between_attention(L + 1, g - 1):
                            source_scores(L + 1, g - 1)
                        if L == 1 and g == 0:
                            for r in range(j * NT // 64, (j + 1) * NT // 64):
                                pe.wait_ge(s_spot, r + 1)
                                if r:
                                    pe.wait_ge(s_place_t, r)
                                for i in range(4):
                                    last = nc.tensor.transpose(TR[:, i * P:(i + 1) * P], spot[:, 4 * (r % 2) + i, :],
                                                               ident[:, :])
                                last.then_inc(s_spot_t, 1)
                    if L < 3:
                        project(L + 1, g)

            pe.wait_ge(s_out, 64 * GROUPS)
            with pe.If(pe.value_load(flag[0:1, 0:1], min_val=0, max_val=1) > 0):
                for L in (2, 3):
                    with pe.Fori(0, NT) as t:
                        pe.wait_ge(d_h, t + (L * NT + 2))
                        nc.tensor.transpose(TR[:, 0:P], H[:, 0, :], ident[:, :]).then_inc(d_pe, 1)
                        pe.wait_ge(d_cp, 2 * t + (2 * (L - 2) * NT + 1))
                        nc.tensor.matmul(WH[0][:, 0:P + 2], h_t[:, 0:P], w_aug[L][:, :], start=True,
                                         stop=True).then_inc(d_pe, 1)

        @block.vector
        def _(dve):
            own = [0]

            def step(ins):
                own[0] += 1
                ins.then_inc(s_own, 1)
                return own[0]

            nc.vector.memset(ones8[:, :], 1.0)
            nc.vector.memset(ring[:, :, :, SEG:SEG + FOUND], 1)
            nc.vector.memset(minus_half[:, :], -0.5)
            nc.vector.memset(eps[:, :], LN_EPS)
            nc.vector.memset(zeros_b[:, :], 0.0)
            nc.vector.memset(ones_b[:, :], 1.0)
            nc.vector.memset(ones_f[:, :], 1.0)
            nc.vector.memset(full_seg[:, :], 0.0)
            nc.vector.memset(pad_zero[:, :], 0.0)
            nc.vector.memset(pad_row[:, :], 0.0)
            v = step(nc.vector.memset(uncovered[:, :, :], 0.0))
            dve.wait_ge(s_own, v)
            nc.vector.memset(pad_row[:, P:P + 1], PAD_SCORE)
            for b in range(TILES):
                nc.vector.memset(uncovered[:, b, SLOTS[b]:KEEP], 1.0)
            nc.vector.memset(rec_out[:, :, KEEP:REC], 0)
            dve.wait_ge(s_iota, 6)
            nc.vector.tensor_scalar(before[:, :], diff[:, :], 0.0, None, ALU.is_gt)
            nc.vector.tensor_copy(places_row[:, :], H[:, :, :].rearrange("p t f -> p (t f)"))
            v = step(nc.vector.tensor_scalar(ident[:, :], diff[:, :], 0.0, None, ALU.is_equal))
            dve.wait_ge(s_own, v)
            nc.vector.tensor_copy(rec_out[:, :, KEEP], target[:, :]).then_inc(s_const, 1)

            def layer_norm(L, g):
                q = made(L, g)

                def scale_rows(c):
                    part = slice(c * QUARTER, (c + 1) * QUARTER)
                    dve.wait_ge(s_std, 4 * q + c + 1)
                    v = step(nc.vector.reciprocal(rstd[:, part], std[:, part]))
                    dve.wait_ge(s_own, v)
                    ins = nc.vector.scalar_tensor_tensor(out=shift[:, part], in0=mean_var[:, part, 0], scalar=-1.0,
                                                         in1=rstd[:, part], op0=ALU.mult, op1=ALU.mult)
                    if L < 2:
                        ins.then_inc(s_ln, 1)
                        return
                    v = step(ins)
                    if c == 0:
                        if q == 2 * GROUPS:
                            dve.wait_ge(s_tab[1], 64 * GROUPS)
                        else:
                            dve.wait_ge(s_tr, 4 * (q - 2 * GROUPS))
                    dve.wait_ge(s_own, v)
                    for t in range(c * QUARTER, (c + 1) * QUARTER):
                        last = nc.vector.tensor_scalar(H[:, t, :], X[:, g * TILES + t, :], rstd[:, t:t + 1],
                                                       shift[:, t:t + 1], ALU.mult, ALU.add)
                    last.then_inc(s_hn, 1)

                def rows_stats(c):
                    if L:
                        dve.wait_ge(s_added, 4 * ((L - 1) * GROUPS + g) + c + 1)
                    for t in range(c * QUARTER, (c + 1) * QUARTER):
                        last = nc.vector.bn_stats(stats[:, t, :], X[:, g * TILES + t, :])
                    return step(last)

                def mean_and_variance(c, v):
                    if c == 0 and 0 < q <= 2 * GROUPS:
                        dve.wait_ge(s_h, 4 * q)
                    dve.wait_ge(s_own, v)
                    for t in range(c * QUARTER, (c + 1) * QUARTER):
                        last = nc.vector.bn_aggr(mean_var[:, t, :], stats[:, t, :])
                    last.then_inc(s_var, 1)

                if L == 0:
                    dve.wait_ge(s_x[g], 16)
                if between_attention(L, g):
                    v = [rows_stats(c) for c in range(4)]
                    for c in range(4):
                        mean_and_variance(c, v[c])
                    for c in range(4):
                        scale_rows(c)
                    return
                for c in range(4):
                    v = rows_stats(c)
                    if L and g == GROUPS - 1 and c < 2:
                        add_quarter(L - 1, g, c + 2)
                    if c:
                        scale_rows(c - 1)
                    mean_and_variance(c, v)
                scale_rows(3)

            at = {}

            def shorten(t, s):
                b = t % TILES
                cand = found[:, t % 2, :]
                if s == 0:
                    dve.wait_ge(s_found, LOADS * (t + 1))
                    at[0] = step(nc.vector.tensor_tensor(key_a[:, :], seg_base[:, :], cand, ALU.subtract))
                elif s == 1:
                    dve.wait_ge(s_own, at[0])
                    at[1] = step(nc.vector.scalar_tensor_tensor(out=key_b[:, :], in0=cand, scalar=float(SEG),
                                                                in1=key_a[:, :], op0=ALU.is_lt, op1=ALU.mult))
                elif s == 2:
                    dve.wait_ge(s_own, at[1])
                    at[2] = step(nc.vector.max(best[:, b, 0:8], key_b[:, :]))
                elif s == 3:
                    dve.wait_ge(s_own, at[2])
                    at[3] = step(nc.vector.match_replace(key_a[:, :], best[:, b, 0:8], key_b[:, :], 0.0))
                elif s == 4:
                    dve.wait_ge(s_own, at[3])
                    last8 = key_b[:, :].rearrange("p (s k) -> p s k", s=SEGS)[:, :, FOUND - 1]
                    nc.vector.tensor_tensor(full_seg[:, :], full_seg[:, :], last8, ALU.max)
                    at[4] = step(nc.vector.max(best[:, b, 8:16], key_a[:, :]))
                elif s == 5:
                    dve.wait_ge(s_own, at[4])
                    at[5] = step(nc.vector.match_replace(key_b[:, :], best[:, b, 8:16], key_a[:, :], 0.0))
                elif s == 6:
                    dve.wait_ge(s_own, at[5])
                    at[6] = step(nc.vector.max(best[:, b, 16:24], key_b[:, :]))

            def search(t, between):
                for s in range(SEGS):
                    h = t * LOADS + s // HALF
                    if s % HALF == 0:
                        dve.wait_ge(s_adj[h % RING], 16 * (h // RING + 1))
                    last = nc.vector.max_index(found[:, t % 2, s * FOUND:(s + 1) * FOUND], ones8[:, :],
                                               ring[:, h % RING, s % HALF, :])
                    if s % HALF == HALF - 1:
                        last.then_inc(s_found, 1)
                    if t % TILES:
                        shorten(t - 1, s)
                    between(s)
                for s in range(SEGS, 7):
                    if t % TILES:
                        shorten(t - 1, s)
                    between(s)

            def sort_rows(g):
                for s in range(7):
                    shorten(g * TILES + TILES - 1, s)
                dve.wait_ge(s_own, at[6])
                v = step(nc.vector.tensor_scalar(cells[:, :, :], best[:, :, :], 0.0, None, ALU.is_gt))
                dve.wait_ge(s_own, v)
                v = step(nc.vector.tensor_reduce(deg[:, :], cells[:, :, :], AX.X, ALU.add))
                dve.wait_ge(s_own, v)
                nc.vector.tensor_scalar(alone[:, g * TILES:(g + 1) * TILES], deg[:, :], 0.0, None, ALU.is_equal)
                nc.vector.tensor_tensor(is_class[:, :, :], class_of[:, :, :],
                                        deg[:, :].unsqueeze(1).broadcast_to([P, CLASSES, TILES]),
                                        ALU.is_equal).then_inc(s_class, 1)
                if g:
                    dve.wait_ge(s_rec, 16 * TILES * g)
                nc.vector.tensor_scalar(rec_out[:, :, 0:KEEP], best[:, :, :], -1.0, float(N), ALU.mult, ALU.add)
                dve.wait_ge(s_counts, g + 1)
                cols = CLASSES * TILES
                v = step(nc.vector.tensor_tensor_scan(ahead[:, :], zeros_b[:, 0:cols], WH[1][:, 0:cols], 0.0,
                                                      ALU.add, ALU.add))
                dve.wait_ge(s_own, v)
                v = step(nc.vector.tensor_tensor(ahead[:, :], ahead[:, :], WH[1][:, 0:cols], ALU.subtract))
                dve.wait_ge(s_own, v)
                v = step(nc.vector.tensor_tensor(ahead[:, :], ahead[:, :], WH[0][:, 0:cols], ALU.add))
                dve.wait_ge(s_own, v)
                v = step(nc.vector.tensor_tensor(picked[:, :, :].rearrange("p d t -> p (d t)"), ahead[:, :],
                                                 is_class[:, :, :].rearrange("p d t -> p (d t)"), ALU.mult))
                dve.wait_ge(s_own, v)
                v = step(nc.vector.tensor_reduce(rank[:, :], picked[:, :, :].rearrange("p d t -> p t d"), AX.X, ALU.add))
                dve.wait_ge(s_own, v)
                v = step(nc.vector.tensor_copy(rank_int[:, :], rank[:, :]))
                dve.wait_ge(s_own, v)
                nc.vector.tensor_scalar(rank_lo[:, :], rank_int[:, :], P - 1, TILES.bit_length() - 1, ALU.bitwise_and,
                                        ALU.logical_shift_left)
                v = step(nc.vector.tensor_scalar(rank_hi[:, :], rank_int[:, :], P.bit_length() - 1, None,
                                                 ALU.logical_shift_right))
                dve.wait_ge(s_own, v)
                v = step(nc.vector.tensor_tensor(rank_at[:, :], rank_lo[:, :], rank_hi[:, :], ALU.bitwise_or))
                dve.wait_ge(s_own, v)
                nc.vector.tensor_scalar(target[:, :], rank_at[:, :], group_base[:, g:g + 1], None,
                                        ALU.add).then_inc(s_target, 1)

            def take_lists(g):
                dve.wait_ge(s_lists, 16 * (g + 1))
                rows = slice(g * TILES, (g + 1) * TILES)
                at["place"] = step(nc.vector.tensor_copy(place[:, rows], lists[:, g, :, KEEP]))
                v = step(nc.vector.scalar_tensor_tensor(out=cells[:, :, :], in0=lists[:, g, :, 0:KEEP],
                                                        scalar=float(N), in1=uncovered[:, :, :], op0=ALU.is_lt,
                                                        op1=ALU.mult))
                for i, (b, k) in enumerate(DEEP_FROM.items()):
                    nc.vector.tensor_reduce(last_in[:, g, i:i + 1], lists[:, g, b, k:SLOTS[b]], AX.X, ALU.min)
                dve.wait_ge(s_own, v)
                return step(nc.vector.tensor_reduce(stair[:, g:g + 1], cells[:, :, :], AX.XY, ALU.max))

            def ways_back(L, g, j):
                if turn(L, g, j) >= AHEAD:
                    wait_back(turn(L, g, j) - AHEAD)
                if ways_by_act(L, j):
                    return
                if L == 0 and j == 0:
                    dve.wait_ge(s_own, at["place"])
                t = g * TILES + ORDER[j]
                nc.vector.tensor_scalar(Q[:, j % AHEAD, :], places_row[:, :], place[:, t:t + 1], None, ALU.is_equal)

            def wait_back(n):
                if n % TILES == TILES - 1:
                    dve.wait_ge(s_bank, 4 * (n // TILES + 1))
                else:
                    dve.wait_ge(s_back, n // TILES * (TILES - 1) + n % TILES + 1)

            def split(L, j, s):
                left, part = rest[:, j % 2, :], parts[:, j % AHEAD, :, :]
                dve.wait_ge(s_own, at["split", j])
                if s == 0:
                    if L < 2:
                        ins = nc.vector.tensor_copy(part[:, 0, :], agg[:, j % 2, :])
                    else:
                        ins = nc.vector.tensor_scalar(part[:, 0, :], num[:, j % 2, :], rden[:, j % 2:j % 2 + 1], None,
                                                      ALU.mult)
                elif s == 1:
                    if L < 2:
                        ins = nc.vector.tensor_tensor(left, agg[:, j % 2, :], part[:, 0, :], ALU.subtract)
                    else:
                        ins = nc.vector.scalar_tensor_tensor(out=left, in0=num[:, j % 2, :],
                                                             scalar=rden[:, j % 2:j % 2 + 1], in1=part[:, 0, :],
                                                             op0=ALU.mult, op1=ALU.subtract)
                elif s == 2:
                    ins = nc.vector.tensor_copy(part[:, 1, :], left)
                else:
                    nc.vector.tensor_tensor(part[:, 2, :], left, part[:, 1, :], ALU.subtract).then_inc(s_agg, 1)
                    return
                at["split", j] = step(ins)

            def arrived(L, g, b):
                so_far = L * GROUPS + g + 1
                first = min(so_far, GROUPS - 1)
                dve.wait_ge(s_gath[b], 16 * (SLOTS[b] * first + slots_of(L, g, b) * (so_far - first)))
                if b in DEEP_FROM and some_deep(L, g):
                    dve.wait_ge(s_deep, so_far - first)

            def reduce_max(L, g, j):
                reduce_only(L, g, j)
                for s in range(4):
                    split(L, j, s)

            def reduce_only(L, g, j):
                ways_back(L, g, j)
                b = ORDER[j]
                arrived(L, g, b)
                at["split", j] = step(nc.vector.tensor_reduce(
                    agg[:, j % 2, :], region(b)[:, :, 0:P].rearrange("p k f -> p f k"), AX.X, ALU.max))

            def add_quarter(L, g, c):
                dve.wait_ge(s_bank, 4 * (L * GROUPS + g) + c + 1)
                rows = X[:, g * TILES + 4 * c:g * TILES + 4 * c + 4, :].rearrange("p t f -> p (t f)")
                if L < 3:
                    ins = nc.vector.tensor_tensor(rows, rows, U[c][:, :], ALU.add)
                else:
                    ins = nc.vector.scalar_tensor_tensor(out=rows, in0=U[c][:, :], scalar=0.0, in1=rows,
                                                         op0=ALU.max, op1=ALU.add)
                ins.then_inc(s_added, 1)

            def add_up(L, g):
                for c in range(2 if L < 3 and g == GROUPS - 1 else 4):
                    add_quarter(L, g, c)
                if between_attention(L + 1, g):
                    first_scores(L, g + 1)
                if L < 3:
                    layer_norm(L + 1, g)

            def reduce_between(g, tiles):
                def between(s):
                    for j in tiles:
                        if s == 1:
                            reduce_only(0, g - 1, j)
                        elif 2 <= s < 6:
                            split(0, j, s - 2)
                return between

            def leave_blank():
                dve.wait_ge(s_agg, turn(0, GROUPS - 1, 0))
                for b, k in DEEP_FROM.items():
                    last = nc.vector.memset(region(b)[:, k:SLOTS[b], :], 0.0)
                v = step(last)
                dve.wait_ge(s_own, v)
                for b, k in DEEP_FROM.items():
                    last = nc.vector.memset(region(b)[:, k:SLOTS[b], P:P + 1], PAD_SCORE)
                last.then_inc(s_blank, 1)

            for g in range(GROUPS):
                for b in range(TILES):
                    search(g * TILES + b, reduce_between(g, range(reduced_after(b - 1), reduced_after(b)) if g else ()))
                    if g == 0 and b % (TILES // GROUPS) == TILES // GROUPS - 1:
                        layer_norm(0, b // (TILES // GROUPS))
                    if g == GROUPS - 1 and reduced_after(b - 1) == TILES > reduced_after(b - 2):
                        leave_blank()
                    if g:
                        if b == 0 and g >= 2:
                            add_up(0, g - 2)
                        if b == 3:
                            take_lists(g - 1)
                sort_rows(g)
            add_up(0, GROUPS - 2)
            v = take_lists(GROUPS - 1)
            dve.wait_ge(s_own, v)

            dve.wait_ge(s_checked, NT * LOADS)
            nc.vector.tensor_reduce(faults[:, 0:1], full_seg[:, :], AX.X, ALU.max)
            nc.vector.tensor_reduce(faults[:, 1:2], stair[:, :], AX.X, ALU.max)
            v = step(nc.vector.tensor_scalar(odd_sums[:, :], sums[:, :], HALF * SEG / 4, None, ALU.not_equal))
            dve.wait_ge(s_own, v)
            v = step(nc.vector.tensor_reduce(faults[:, 2:3], odd_sums[:, :], AX.X, ALU.max))
            dve.wait_ge(s_own, v)
            v = step(nc.vector.tensor_reduce(least_in[:, :], last_in[:, :, :], AX.X, ALU.min))
            nc.vector.tensor_reduce(fault[:, 0:1], faults[:, 0:3], AX.X, ALU.max)
            dve.wait_ge(s_own, v)
            nc.vector.tensor_tensor(least_two[:, 0:1], least_in[:, 0:1], least_in[:, GROUPS - 1:GROUPS], ALU.min)
            v = step(nc.vector.tensor_tensor(least_two[:, 1:GROUPS], least_in[:, 1:GROUPS], least_in[:, 0:GROUPS - 1],
                                             ALU.min))
            dve.wait_ge(s_own, v)
            nc.vector.tensor_scalar(fault[:, 1:1 + GROUPS], least_two[:, :], float(N), None, ALU.is_lt).then_inc(s_flt, 1)
            places = lists[:, :, :, KEEP].rearrange("p g t -> p (g t)")
            nc.vector.tensor_scalar(place_lo[:, :], places, P - 1, None, ALU.bitwise_and)
            v = step(nc.vector.tensor_scalar(place_hi[:, :], places, P.bit_length() - 1, None, ALU.logical_shift_right))
            dve.wait_ge(s_own, v)
            nc.vector.tensor_copy(in_tile[:, :], place_lo[:, :])
            v = step(nc.vector.tensor_copy(tile_no[:, :], place_hi[:, :]))
            dve.wait_ge(s_own, v)
            nc.vector.tensor_tensor(tile_of[:, :, :], places_row[:, 0:TILES].unsqueeze(1).broadcast_to([P, NT, TILES]),
                                    tile_no[:, :].unsqueeze(2).broadcast_to([P, NT, TILES]), ALU.is_equal)
            nc.vector.memset(wh_rows[:, :, P + 2:ROW], 0.0)
            dve.wait_ge(s_fltsum, 1)
            nc.vector.tensor_scalar(flag[:, :], MEAN[:, 0:1 + GROUPS], 0.0, None, ALU.is_gt).then_inc(s_flag, 1)

            for j in range(TILES):
                reduce_max(0, GROUPS - 1, j)
            add_up(0, GROUPS - 1)

            def score(L, g, j):
                b = ORDER[j]
                k, t = SLOTS[b], g * TILES + b
                arrived(L, g, b)
                at["score"] = step(nc.vector.tensor_scalar(scores[:, j % 2, 0:k], region(b)[:, :, P], e1[:, t:t + 1],
                                                           None, ALU.add))

            def leak(L, g, j):
                k, r = SLOTS[ORDER[j]], j % 2
                dve.wait_ge(s_own, at["score"])
                at["leaky"] = step(nc.vector.scalar_tensor_tensor(out=leaky[:, r, 0:k], in0=scores[:, r, 0:k],
                                                                  scalar=SLOPE[L], in1=scores[:, r, 0:k],
                                                                  op0=ALU.mult, op1=ALU.max))

            def largest(L, g, j):
                k, r = SLOTS[ORDER[j]], j % 2
                dve.wait_ge(s_own, at["leaky"])
                nc.vector.tensor_reduce(neg_max[:, r:r + 1], leaky[:, r, 0:k], AX.X, ALU.max,
                                        negate=True).then_inc(s_scores, 1)

            def first_scores(L, g):
                score(L, g, 0)
                leak(L, g, 0)
                largest(L, g, 0)

            def lonely(L, g, j):
                t = g * TILES + j
                at["lonely"] = step(nc.vector.scalar_tensor_tensor(
                    out=X[:, t, :], in0=mean_wh[:, :], scalar=alone[:, t:t + 1], in1=X[:, t, :],
                    op0=ALU.mult, op1=ALU.add))

            def attend(L, g, j):
                b = ORDER[j]
                k, r, rows = SLOTS[b], j % 2, region(b)[:, :, 0:P]
                ahead = j + 1 < TILES
                if ahead:
                    score(L, g, j + 1)
                if j:
                    ways_back(L, g, j - 1)
                    split(L, j - 1, 0)
                if ahead:
                    leak(L, g, j + 1)
                if j:
                    split(L, j - 1, 1)
                if ahead:
                    largest(L, g, j + 1)
                if j:
                    split(L, j - 1, 2)
                dve.wait_ge(s_prob, turn(L - 2, g, j) + 1)
                nc.vector.reciprocal(rden[:, r:r + 1], den[:, r:r + 1])
                if j:
                    split(L, j - 1, 3)
                v = step(nc.vector.tensor_tensor(rows, rows, prob[:, r, 0:k].unsqueeze(2).broadcast_to([P, k, P]),
                                                 ALU.mult))
                lonely(L, g, j)
                dve.wait_ge(s_own, v)
                at["split", j] = step(nc.vector.tensor_reduce(num[:, r, :], rows.rearrange("p k f -> p f k"), AX.X, ALU.add))
                if not ahead:
                    ways_back(L, g, j)
                    for s in range(4):
                        split(L, j, s)

            def pick_scores(L, g):
                dve.wait_ge(s_e1, (L - 2) * GROUPS + g + 1)
                rows = slice(g * TILES, (g + 1) * TILES)
                v = step(nc.vector.tensor_tensor(e1_pick[:, rows, :], tile_of[:, rows, :],
                                                 TR[:, 0:TILES * TILES].rearrange("p (t a) -> p t a", a=TILES), ALU.mult))
                dve.wait_ge(s_own, v)
                nc.vector.tensor_reduce(e1[:, rows], e1_pick[:, rows, :], AX.X, ALU.add).then_inc(s_e1used, 1)

            for L in range(1, LAYERS):
                if L >= 2:
                    pick_scores(L, GROUPS - 1)
                    dve.wait_ge(s_e1used, (L - 1) * GROUPS)
                    dve.wait_ge(s_mean, 4 * (L - 1) * GROUPS)
                    v = step(nc.vector.tensor_scalar(mean_wh[:, :], MEAN[:, 0:P], 1.0 / N, 0.0 if L == 3 else None, ALU.mult,
                                                     ALU.max if L == 3 else ALU.bypass))
                    dve.wait_ge(s_own, v)
                    dve.sem_inc(s_meanused, 1)
                for g in range(GROUPS):
                    for j in range(TILES):
                        if L < 3 and g and j == TILES // 2:
                            pick_scores(L + 1, g - 1)
                        if L == 1:
                            reduce_max(L, g, j)
                            if g == 0:
                                for r in range(j * NT // 64, (j + 1) * NT // 64):
                                    if r >= 2:
                                        dve.wait_ge(s_spot_t, r - 1)
                                    for i in range(4):
                                        last = nc.vector.tensor_scalar(
                                            spot[:, 4 * (r % 2) + i, :], places_row[:, 0:P],
                                            in_tile[:, 4 * r + i:4 * r + i + 1], None, ALU.is_equal)
                                    last.then_inc(s_spot, 1)
                        else:
                            if j == 0 and not (g and between_attention(L + 1, g - 1)):
                                first_scores(L, g)
                            attend(L, g, j)
                    if L >= 2:
                        dve.wait_ge(s_own, at["lonely"])
                    add_up(L, g)

            dve.wait_ge(s_out, 64 * GROUPS)
            with dve.If(dve.value_load(flag[0:1, 0:1], min_val=0, max_val=1) > 0):
                for s in (d_tile, *d_used):
                    dve.sem_inc(s, 1)
                dve.wait_ge(d_x, 16)
                for L in range(LAYERS):
                    with dve.Fori(0, NT) as t:
                        dve.wait_ge(d_h, t + (L * NT + 1))
                        nc.vector.bn_stats(stats[:, 0, :], X[:, bass.ds(t, 1), :])
                        dve.drain()
                        nc.vector.bn_aggr(mean_var[:, 0, :], stats[:, 0, :]).then_inc(d_var, 1)
                        dve.wait_ge(d_std, t + (L * NT + 1))
                        nc.vector.reciprocal(rstd[:, 0:1], std[:, 0:1])
                        dve.drain()
                        nc.vector.scalar_tensor_tensor(out=shift[:, 0:1], in0=mean_var[:, 0, 0:1], scalar=-1.0,
                                                       in1=rstd[:, 0:1], op0=ALU.mult, op1=ALU.mult).then_inc(d_ln, 1)
                    dve.wait_ge(d_tab, 16 * tab_count(L, NT))
                    if L >= 2:
                        nc.vector.memset(mean_wh[:, 0:1], FILL[L])
                        dve.wait_ge(d_e2, 16 * (L - 1))
                    with dve.Fori(0, NT) as t:
                        dve.wait_ge(d_adj, 16 * t + 16 * (L * NT + 1))
                        if L < 2:
                            nc.vector.tensor_scalar(d_weight, d_edges, 0.0, None, ALU.not_equal)
                        else:
                            nc.vector.tensor_scalar(d_weight, d_target, e1_by_row[:, bass.ds(t, 1)], None, ALU.add)
                            nc.vector.tensor_scalar(d_edges, d_edges, 0.0, None, ALU.is_le)
                            dve.drain()
                            nc.vector.scalar_tensor_tensor(out=d_weight, in0=d_weight, scalar=SLOPE[L], in1=d_weight,
                                                           op0=ALU.mult, op1=ALU.max)
                            dve.drain()
                            nc.vector.copy_predicated(d_weight, d_edges, mean_wh[:, 0:1].broadcast_to([P, N]))
                            dve.drain()
                            nc.vector.tensor_reduce(neg_max[:, 0:1], d_weight, AX.X, ALU.max,
                                                    negate=True).then_inc(d_scores, 1)
                            dve.wait_ge(d_prob, t + ((L - 2) * NT + 1))
                            nc.vector.reciprocal(rden[:, 0:1], den[:, 0:1])
                        nc.vector.memset(num[:, 0, :], 0.0)
                        dve.drain()
                        how = ALU.max if L < 2 else ALU.add
                        with dve.Fori(0, PAIRS) as c:
                            for i in range(2):
                                dve.wait_ge(d_rows[i], 16 * (t * PAIRS + c) + 16 * (L * NT * PAIRS + 1))
                                part = d_weight[:, bass.ds(c * (2 * CHUNK) + i * CHUNK, CHUNK)]
                                nc.vector.tensor_tensor(d_prod, d_chunk[i],
                                                        part.unsqueeze(2).broadcast_to([P, CHUNK, P]),
                                                        ALU.mult).then_inc(d_used[i], 1)
                                dve.drain()
                                nc.vector.tensor_reduce(agg[:, 0, :], d_prod.rearrange("p k f -> p f k"), AX.X, how)
                                dve.drain()
                                nc.vector.tensor_tensor(num[:, 0, :], num[:, 0, :], agg[:, 0, :], how)
                                dve.drain()
                        if L >= 2:
                            nc.vector.tensor_scalar(num[:, 0, :], num[:, 0, :], rden[:, 0:1], 0.0 if L == 3 else None,
                                                    ALU.mult, *([ALU.max] if L == 3 else []))
                            dve.drain()
                        rows = X[:, bass.ds(t, 1), :].rearrange("p t f -> p (t f)")
                        nc.vector.tensor_tensor(rows, rows, num[:, 0, :], ALU.add).then_inc(d_tile, 1)
                    dve.drain()


def kernel(x, adj, L2_gnn_Ws, L2_gnn_a, L3_gnn_W, L3_gnn_a):
    import numpy as _np
    import concourse.bacc as _bacc
    from concourse import mybir as _mybir
    from concourse.bass_utils import run_bass_kernel_spmd as _run

    nc = _bacc.Bacc("TRN2", target_bir_lowering=False, num_devices=1)
    arrays, args = {}, []
    for name, a in (("x", x), ("adj", adj), ("w2", L2_gnn_Ws), ("a2", L2_gnn_a), ("w3", L3_gnn_W), ("a3", L3_gnn_a)):
        a = _np.ascontiguousarray(a)
        arrays[f"in_{name}"] = a
        args.append(nc.dram_tensor(f"in_{name}", a.shape, _mybir.dt.from_np(a.dtype), kind="ExternalInput").ap())
    args.append(nc.dram_tensor("out_h", tuple(x.shape), _mybir.dt.float32, kind="ExternalOutput").ap())
    gnn_kernel(nc, *args)
    return _run(nc, [arrays], core_ids=[0]).results[0]["out_h"]
```
